# Optimizing a Trainium2 kernel written in Bass

```python
import numpy as np
import jax
import jax.numpy as jnp

def _softmax(x, axis=-1):
    return jax.nn.softmax(x, axis=axis)

def _gelu(x):
    return jax.nn.gelu(x, approximate=True)

def _silu(x):
    return jax.nn.silu(x)

def _sigmoid(x):
    return jax.nn.sigmoid(x)

def _layernorm(x, axis=-1, eps=1e-05):
    m = jnp.mean(x, axis=axis, keepdims=True)
    v = jnp.var(x, axis=axis, keepdims=True)
    return (x - m) / jnp.sqrt(v + eps)

def _scatter_add(tgt, idx, src, axis=0):
    return tgt.at[idx].add(src)

def _segment_sum(src, seg, n):
    return jax.ops.segment_sum(src, seg, n)
kernel_name = 'mk_vit_tower_d1_tok_img256_r4_701a72'

def setup_inputs(seed: int=0):
    np.random.seed(seed)
    _w = jnp.asarray

    def _rec_inputs():
        import jax
        import jax.numpy as jnp
        _rk = jax.random.key(seed)
        x = 7.22013e-05 + 1.00017 * jax.random.normal(jax.random.fold_in(_rk, 1), (2, 1, 1024, 64), jnp.float32)
        return x
    x = _rec_inputs()

    def _L0_tok_setup():
        import jax, jax.numpy as jnp
        import numpy as np
        T, D_IN, D_INT, D_OUT, B = (1024, 64, 64, 64, 8)
        key = jax.random.key(seed)
        ks = jax.random.split(key, 12)
        s_in = 1.0 / np.sqrt(D_IN)
        s_int = 1.0 / np.sqrt(D_INT)
        return {'x_batched': jax.random.normal(ks[0], (B, 1, T, D_IN), dtype=jnp.float32), 'd_gamma_batched': jax.random.uniform(ks[1], (T, T), dtype=jnp.float32), 'Wq': jax.random.uniform(ks[2], (D_IN, D_INT), jnp.float32, -s_in, s_in), 'bq': jax.random.uniform(ks[3], (D_INT,), jnp.float32, -s_in, s_in), 'Wk': jax.random.uniform(ks[4], (D_IN, D_INT), jnp.float32, -s_in, s_in), 'bk': jax.random.uniform(ks[5], (D_INT,), jnp.float32, -s_in, s_in), 'Wv': jax.random.uniform(ks[6], (D_IN, D_INT), jnp.float32, -s_in, s_in), 'bv': jax.random.uniform(ks[7], (D_INT,), jnp.float32, -s_in, s_in), 'Wo': jax.random.uniform(ks[8], (D_INT, D_OUT), jnp.float32, -s_int, s_int), 'bo': jax.random.uniform(ks[9], (D_OUT,), jnp.float32, -s_int, s_int), 'prelu_a': jnp.float32(0.25)}
    _L0_tok_all = _L0_tok_setup()
    _L0_tok_in = {k: v for k, v in _L0_tok_all.items() if k in ('d_gamma_batched', 'Wq', 'bq', 'Wk', 'bk', 'Wv', 'bv', 'Wo', 'bo', 'prelu_a')}
    del _L0_tok_all

    def _L0_attn_setup():
        import jax, jax.numpy as jnp
        import numpy as np
        U_DECAY = 0.97
        X_DECAY = 0.97
        LN_EPS = 1e-05
        L1_EPS = 1e-12

        def _ln(x):
            m = jnp.mean(x, axis=-1, keepdims=True)
            v = jnp.mean((x - m) ** 2, axis=-1, keepdims=True)
            return (x - m) * jax.lax.rsqrt(v + LN_EPS)
        key = jax.random.key(seed)
        k0, k1, k2, k3 = jax.random.split(key, 4)
        B, T, d, n = (8, 64, 64, 256)
        embeddings = jax.random.normal(k0, (B, T, d), dtype=jnp.float32)
        E = jax.random.normal(k1, (d, n), dtype=jnp.float32) / n ** 0.5
        Dx = jax.random.normal(k2, (n, d), dtype=jnp.float32) / d ** 0.5
        Dy = jax.random.normal(k3, (n, d), dtype=jnp.float32) / d ** 0.5
        return {'embeddings': embeddings, 'E': E, 'Dx': Dx, 'Dy': Dy}
    _L0_attn_all = _L0_attn_setup()
    _L0_attn_in = {k: v for k, v in _L0_attn_all.items() if k in ('E', 'Dx', 'Dy')}
    del _L0_attn_all

    def _L0_ffn_setup():
        import math
        import jax, jax.numpy as jnp
        import numpy as np
        CAPACITY_FACTOR = 1.25
        key = jax.random.key(seed)
        ks = jax.random.split(key, 5)
        B, L, D, F, E = (8, 2048, 64, 256, 8)
        h = jax.random.normal(ks[0], (B, L, D), dtype=jnp.float32)
        gate_w = jax.random.normal(ks[1], (D, E), dtype=jnp.float32) * 0.02
        gate_b = jnp.zeros((E,), dtype=jnp.float32)
        w1 = jax.random.normal(ks[2], (E, D, F), dtype=jnp.float32) * (1.0 / math.sqrt(D))
        b1 = jnp.zeros((E, F), dtype=jnp.float32)
        w2 = jax.random.normal(ks[3], (E, F, D), dtype=jnp.float32) * (1.0 / math.sqrt(F))
        b2 = jnp.zeros((E, D), dtype=jnp.float32)
        return {'h': h, 'gate_w': gate_w, 'gate_b': gate_b, 'w1': w1, 'b1': b1, 'w2': w2, 'b2': b2}
    _L0_ffn_all = _L0_ffn_setup()
    _L0_ffn_in = {k: v for k, v in _L0_ffn_all.items() if k in ('gate_w', 'gate_b', 'w1', 'b1', 'w2', 'b2')}
    del _L0_ffn_all
    return {'x': x, 'L0_tok_d_gamma_batched': _L0_tok_in['d_gamma_batched'], 'L0_tok_Wq': _L0_tok_in['Wq'], 'L0_tok_bq': _L0_tok_in['bq'], 'L0_tok_Wk': _L0_tok_in['Wk'], 'L0_tok_bk': _L0_tok_in['bk'], 'L0_tok_Wv': _L0_tok_in['Wv'], 'L0_tok_bv': _L0_tok_in['bv'], 'L0_tok_Wo': _L0_tok_in['Wo'], 'L0_tok_bo': _L0_tok_in['bo'], 'L0_tok_prelu_a': _L0_tok_in['prelu_a'], 'L0_attn_E': _L0_attn_in['E'], 'L0_attn_Dx': _L0_attn_in['Dx'], 'L0_attn_Dy': _L0_attn_in['Dy'], 'L0_ffn_gate_w': _L0_ffn_in['gate_w'], 'L0_ffn_gate_b': _L0_ffn_in['gate_b'], 'L0_ffn_w1': _L0_ffn_in['w1'], 'L0_ffn_b1': _L0_ffn_in['b1'], 'L0_ffn_w2': _L0_ffn_in['w2'], 'L0_ffn_b2': _L0_ffn_in['b2']}

def reference(x, L0_tok_d_gamma_batched, L0_tok_Wq, L0_tok_bq, L0_tok_Wk, L0_tok_bk, L0_tok_Wv, L0_tok_bv, L0_tok_Wo, L0_tok_bo, L0_tok_prelu_a, L0_attn_E, L0_attn_Dx, L0_attn_Dy, L0_ffn_gate_w, L0_ffn_gate_b, L0_ffn_w1, L0_ffn_b1, L0_ffn_w2, L0_ffn_b2):
    import jax
    import jax.numpy as jnp

    def _L0_tok_ref(x_batched, d_gamma_batched, Wq, bq, Wk, bk, Wv, bv, Wo, bo, prelu_a):
        import jax, jax.numpy as jnp
        import numpy as np
        T, D_IN, D_INT, D_OUT, B = (1024, 64, 64, 64, 8)
        x = x_batched.reshape(x_batched.shape[0], T, D_IN)
        q = x @ Wq + bq
        k = x @ Wk + bk
        v = x @ Wv + bv
        scores = jnp.einsum('btd,bsd->bts', q, k)
        retained = jnp.einsum('bts,bsd->btd', d_gamma_batched * scores, v)
        y = retained @ Wo + bo
        out = jnp.where(y >= 0, y, prelu_a * y)
        return out

    def _L0_attn_ref(embeddings, E, Dx, Dy):
        import jax, jax.numpy as jnp
        import numpy as np
        U_DECAY = 0.97
        X_DECAY = 0.97
        LN_EPS = 1e-05
        L1_EPS = 1e-12

        def _ln(x):
            m = jnp.mean(x, axis=-1, keepdims=True)
            v = jnp.mean((x - m) ** 2, axis=-1, keepdims=True)
            return (x - m) * jax.lax.rsqrt(v + LN_EPS)
        B, T, d = embeddings.shape
        n = E.shape[1]

        def step(carry, v_prev):
            x_state, rho = carry
            x_update = jax.nn.relu(v_prev @ Dx.T)
            x_t = X_DECAY * x_state + x_update
            x_t = x_t / jnp.maximum(jnp.sum(jnp.abs(x_t), axis=-1, keepdims=True), L1_EPS)
            a_star = jnp.einsum('bdn,bn->bd', rho, x_t)
            y_core = _ln(a_star) @ Dy.T
            y_t = jax.nn.relu(y_core) * jax.nn.relu(x_t)
            v_star = _ln(y_t @ E.T)
            rho_t = U_DECAY * rho + _ln(v_prev)[:, :, None] * x_t[:, None, :]
            return ((x_t, rho_t), v_star)
        x0 = jnp.zeros((B, n), dtype=embeddings.dtype)
        rho0 = jnp.zeros((B, d, n), dtype=embeddings.dtype)
        _, vs = jax.lax.scan(step, (x0, rho0), jnp.swapaxes(embeddings, 0, 1))
        return jnp.swapaxes(vs, 0, 1)

    def _L0_ffn_ref(h, gate_w, gate_b, w1, b1, w2, b2):
        import math
        import jax, jax.numpy as jnp
        import numpy as np
        CAPACITY_FACTOR = 1.25
        B, L, D = h.shape
        E = gate_w.shape[1]
        T = B * L
        C = max(1, math.ceil(CAPACITY_FACTOR * T / E))
        x = h.reshape(T, D)
        logits = x @ gate_w + gate_b
        probs = jax.nn.softmax(logits, axis=-1)
        idx = jnp.argmax(probs, axis=-1)
        prb = jnp.take_along_axis(probs, idx[:, None], axis=1)[:, 0]
        one_hot = jax.nn.one_hot(idx, E, dtype=jnp.float32)
        pos = (jnp.cumsum(one_hot, axis=0) * one_hot).sum(-1).astype(jnp.int32) - 1
        kept = pos < C
        pos_safe = jnp.where(kept, pos, C)
        buf = jnp.zeros((E, C, D), dtype=h.dtype).at[idx, pos_safe].set(x, mode='drop')
        hmid = jax.nn.relu(jnp.einsum('ecd,edf->ecf', buf, w1) + b1[:, None, :])
        ybuf = jnp.einsum('ecf,efd->ecd', hmid, w2) + b2[:, None, :]
        pos_g = jnp.minimum(pos, C - 1)
        y_tok = ybuf[idx, pos_g] * (prb * kept)[:, None]
        y = y_tok.reshape(B, L, D)
        y = jnp.nan_to_num(y, nan=0.0, posinf=10000.0, neginf=-10000.0)
        return y
    h = _L0_tok_ref(x, L0_tok_d_gamma_batched, L0_tok_Wq, L0_tok_bq, L0_tok_Wk, L0_tok_bk, L0_tok_Wv, L0_tok_bv, L0_tok_Wo, L0_tok_bo, L0_tok_prelu_a)
    h = h + _L0_attn_ref(_layernorm(h, axis=-1), L0_attn_E, L0_attn_Dx, L0_attn_Dy)
    h = h + _L0_ffn_ref(_layernorm(h, axis=-1), L0_ffn_gate_w, L0_ffn_gate_b, L0_ffn_w1, L0_ffn_b1, L0_ffn_w2, L0_ffn_b2)
    return h

_drawn_inputs = setup_inputs


def setup_inputs(seed=0):
    import zlib

    import numpy as np

    out = dict(_drawn_inputs(seed))
    spreads = {'L0_ffn_gate_b': (0.0, 0.8), 'L0_ffn_b1': (0.0, 0.8), 'L0_ffn_b2': (0.0, 0.8)}
    factors = {'L0_tok_bo': 8.0,
     'L0_attn_E': 3.019,
     'L0_attn_Dx': 3.621,
     'L0_attn_Dy': 3.643,
     'L0_ffn_gate_w': 8.0,
     'L0_ffn_w1': 8.0,
     'L0_ffn_w2': 8.0}
    for name, (base, spread) in spreads.items():
        noise = np.random.default_rng([zlib.crc32(name.encode()), seed]).standard_normal(out[name].shape)
        drawn = base * np.exp(spread * noise) if base else spread * noise
        out[name] = jnp.asarray(drawn.astype(out[name].dtype))
    for name, factor in factors.items():
        out[name] = (out[name] * factor).astype(out[name].dtype)
    return out
```

```python
import concourse.bass as bass
from concourse import mybir
from contextlib import ExitStack

B, T, D = 2, 1024, 64
N = 256
NE, F = 8, 256
P = 128
NT = T // P
HALF = T // 2
CAP = (5 * B * T) // (4 * NE)
SLOTS = NE * CAP
KS = CAP // 64
PAIRS = NE // 2
DECAY = 0.97
TILE_DECAY = DECAY ** P
LN_EPS, L1_EPS = 1e-5, 1e-12
BIG = 1e35

PARAMS = [("wo", D), ("bo", D), ("dxt", N), ("dyt", N), ("et", 2 * D), ("a", 1), ("b1", 2 * NE), ("b2", PAIRS * D)]
CONSTS = [("ident", P), ("ident97", P), ("upper", P), ("tri", P), ("near", P), ("prev", P),
          ("grow", 1), ("decay", 1), ("first", NT * NE), ("base", NT * NE)]


def columns(table):
    at, out = 0, {}
    for name, width in table:
        out[name] = (at, at + width)
        at += width
    return out, at


PCOL, PWIDTH = columns(PARAMS)
CCOL, CWIDTH = columns(CONSTS)


def build(nc, xT, wa, gammaT, params, consts, gate, w1, w2, out, slots_in, slots_out):
    f32, bf16, i32 = mybir.dt.float32, mybir.dt.bfloat16, mybir.dt.int32
    ALU = mybir.AluOpType
    ACT = mybir.ActivationFunctionType
    AX = mybir.AxisListType.X

    ctx = ExitStack()
    with ctx:
        def sb(name, shape, dt=f32):
            return ctx.enter_context(nc.sbuf_tensor(name, shape, dt))

        def pb(name, shape, dt=f32):
            return ctx.enter_context(nc.psum_tensor(name, shape, dt))

        def sem(name):
            return ctx.enter_context(nc.semaphore(name))

        def both(name, shape, dt=f32):
            return [sb(f"{name}_{b}", shape, dt) for b in range(B)]

        def shared(name, shape, dt=f32):
            return [sb(name, shape, dt)] * B

        x_sb = both("x_sb", [D + 1, T])
        wa_sb = sb("wa_sb", [D + 1, 5 * D])
        gam = sb("gam", [P, NT, T])
        par = sb("par", [P, PWIDTH])
        cst = sb("cst", [P, CWIDTH])
        gate_sb = sb("gate_sb", [D + 1, NE])
        w1_sb = sb("w1_sb", [D, NE, F])
        w2_sb = sb("w2_sb", [P, NE, 2, D])
        ones = sb("ones", [P, 1])
        big = sb("big", [P, P])
        zeros = sb("zeros", [P, SLOTS * D // P])
        tri_bf = sb("tri_bf", [P, P], bf16)
        ones_bf = sb("ones_bf", [P, P], bf16)
        etc = sb("etc", [P, 2, D])
        et_mean = sb("et_mean", [P, 2])

        q_sb = shared("q_sb", [P, T])
        k_sb = shared("k_sb", [P, T])
        v_sb = shared("v_sb", [P, NT, D])
        NG = 6
        gs = sb("gs", [P, NG, HALF])
        ret = shared("ret", [P, HALF])
        y1 = shared("y1", [P, NT, D])
        y2 = shared("y2", [P, NT, D])
        h = shared("h", [P, NT, D])
        hc = shared("hc", [P, NT, D])
        sq = shared("sq", [P, NT, D])
        vn = shared("vn", [P, NT, D])
        lb = shared("lb", [P, NT, D])
        lbc = shared("lbc", [P, NT, D])
        vT = shared("vT", [D, T])
        w = shared("w_all", [P, 2, T])
        wT = shared("wT", [P, NT, 2 * P])
        att = shared("att", [P, NT, P])
        state = shared("state", [P, NT, 2 * D])
        aT = shared("aT", [P, HALF])
        aT2 = shared("aT2", [P, HALF])
        yT = shared("yT", [P, 2, T])
        pq = shared("pq", [P, NT, D])
        h2c = both("h2c", [P, NT, D])
        h3 = both("h3", [P, NT, D])
        h3T = shared("h3T", [D + 1, T])
        lg = both("lg", [P, NT, NE])
        ex = both("ex", [P, NT, NE])
        key = both("key", [P, NT, NE])
        oh = both("oh", [P, NT, NE], bf16)
        slot_i = both("slot_i", [P, NT], i32)
        yg = both("yg", [P, NT, D])
        NC = 40
        col_sb = both("col_sb", [P, NC, NT])
        xb = sb("xb", [P, PAIRS, KS, D])
        xbT = sb("xbT", [D, PAIRS, KS, 2, D])
        hm = sb("hm", [P, 2, 2, 2, CAP])
        yb_sb = sb("yb_sb", [P, PAIRS, KS, D])
        fin = both("fin", [P, NT, D])
        fpos = sb("fpos", [P, 4, D])
        fmask = sb("fmask", [P, 4, D], i32)
        frep = sb("frep", [P, 4, D])

        S = [pb(f"S{i}", [P, HALF]) for i in range(3)]
        R = pb("R", [P, HALF])
        M0 = pb("M0", [P, HALF])
        M3 = pb("M3", [P, HALF])
        AB = pb("AB", [P, T])
        ABh = [AB[:, 0:HALF], AB[:, HALF:T]]

        def pcol(name, lo=0, hi=P):
            a, z = PCOL[name]
            return par[lo:hi, a:z]

        def ccol(name):
            a, z = CCOL[name]
            return cst[:, a:z]

        def ts(j):
            return slice(j * P, (j + 1) * P)

        def hs(i):
            return slice(i * HALF, (i + 1) * HALF)

        def over(col, n):
            return col.unsqueeze(2).to_broadcast([P, NT, n])

        d_x = [sem(f"d_x{b}") for b in range(B)]
        d_wa, d_par, d_cst, d_gate, d_w1, d_w2 = (sem(n) for n in ("d_wa", "d_par", "d_cst", "d_gate", "d_w1", "d_w2"))
        d_gam = [sem(f"d_gam{i}") for i in range(NT)]
        d_zero, d_scatter, d_out = sem("d_zero"), sem("d_scatter"), sem("d_out")
        d_xb = [sem(f"d_xb{p}") for p in range(PAIRS)]
        d_yb = sem("d_yb")
        d_gather = [[sem(f"d_gather{b}_{g}") for g in range(2)] for b in range(B)]
        s_set = sem("s_set")
        s_bfc = sem("s_bfc")
        s_etc = sem("s_etc")
        s_proj, s_projev = sem("s_proj"), sem("s_projev")
        s_score, s_gs, s_gv = sem("s_score"), sem("s_gs"), sem("s_gv")
        s_ret, s_mix, s_y = sem("s_ret"), sem("s_mix"), sem("s_y")
        s_hc, s_hsq = sem("s_hc"), sem("s_hsq")
        s_var = [sem(f"s_var{k}") for k in range(5)]
        s_root = [sem(f"s_root{k}") for k in range(5)]
        s_vn, s_vt, s_vtev = sem("s_vn"), sem("s_vt"), sem("s_vtev")
        s_dx, s_u = sem("s_dx"), sem("s_u")
        s_usum, s_cm, s_m, s_beta = sem("s_usum"), sem("s_cm"), sem("s_m"), sem("s_beta")
        s_abc, s_w = sem("s_abc"), sem("s_w")
        s_cl, s_lb = sem("s_cl"), sem("s_lb")
        s_at, s_att = sem("s_at"), sem("s_att")
        s_wt, s_wtev = sem("s_wt"), sem("s_wtev")
        s_c, s_st = sem("s_c"), sem("s_st")
        s_a, s_aev = sem("s_a"), sem("s_aev")
        s_sa, s_saev = sem("s_sa"), sem("s_saev")
        s_dy, s_yy = sem("s_dy"), sem("s_yy")
        s_q, s_qsq, s_p = sem("s_q"), sem("s_qsq"), sem("s_p")
        s_h2, s_h2sq, s_h3 = sem("s_h2"), sem("s_h2sq"), sem("s_h3")
        s_h3t, s_h3tev = sem("s_h3t"), sem("s_h3tev")
        s_lg, s_lgev, s_dl, s_ex = sem("s_lg"), sem("s_lgev"), sem("s_dl"), sem("s_ex")
        s_oh, s_cum, s_cumev, s_slot = sem("s_oh"), sem("s_cum"), sem("s_cumev"), sem("s_slot")
        s_xt, s_xtev = sem("s_xt"), sem("s_xtev")
        s_up, s_hma, s_hmd = sem("s_up"), sem("s_hma"), sem("s_hmd")
        s_dn, s_yb = sem("s_dn"), sem("s_yb")
        s_fin = sem("s_fin")
        s_chain = sem("s_chain")
        s_pchain = sem("s_pchain")

        SET_ZERO, SET_BIG, SET_ROWS, SET_YG = 1, 3, 4, 6
        block = ctx.enter_context(nc.Block())

        @block.sync
        def _(sp):
            sp.dma_start(wa_sb[:, :], wa).then_inc(d_wa, 16)
            sp.dma_start(x_sb[0][:, :], xT[0]).then_inc(d_x[0], 16)
            for i in range(2):
                sp.dma_start(gam[:, i, :], gammaT[i]).then_inc(d_gam[i], 16)
            sp.dma_start(par[:, :], params).then_inc(d_par, 16)
            for i in range(2, NT):
                sp.dma_start(gam[:, i, :], gammaT[i]).then_inc(d_gam[i], 16)
            sp.dma_start(cst[:, :], consts).then_inc(d_cst, 16)
            sp.dma_start(x_sb[1][:, :], xT[1]).then_inc(d_x[1], 16)
            sp.dma_start(gate_sb[:, :], gate).then_inc(d_gate, 16)
            sp.dma_start(w1_sb[:, :, :], w1.rearrange("e d f -> d e f")).then_inc(d_w1, 16)
            sp.dma_start(w2_sb[:, :, :, :], w2.rearrange("e (c p) d -> p e c d", c=2)).then_inc(d_w2, 16)
            sp.wait_ge(s_set, SET_ZERO)
            sp.dma_start(slots_in.rearrange("(p r) d -> p (r d)", p=P), zeros[:, :]).then_inc(d_zero, 16)
            sp.wait_ge(d_scatter, 16 * B * NT)
            src = slots_in.rearrange("(g e p k) d -> g e p (k d)", g=2, e=PAIRS, p=64)
            for p in range(PAIRS):
                for g in range(2):
                    sp.dma_start(xb[64 * g:64 * g + 64, p, :, :].rearrange("p k d -> p (k d)"), src[g, p]).then_inc(d_xb[p], 16)
            dst = slots_out.rearrange("(g e p k) d -> g e p (k d)", g=2, e=PAIRS, p=64)
            for p in range(PAIRS):
                sp.wait_ge(s_yb, p + 1)
                for g in range(2):
                    sp.dma_start(dst[g, p], yb_sb[64 * g:64 * g + 64, p, :, :].rearrange("p k d -> p (k d)")).then_inc(d_yb, 16)
            for b in range(B):
                for g in range(2):
                    sp.wait_ge(s_fin, 2 * b + g + 1)
                    sp.dma_start(out[b, g * HALF:(g + 1) * HALF, :].rearrange("(j p) d -> p j d", p=P),
                                 fin[b][:, 4 * g:4 * g + 4, :]).then_inc(d_out, 16)
            sp.wait_ge(d_out, 16 * 2 * B)

        @block.gpsimd
        def _(pool):
            nc.gpsimd.memset(zeros[:, :], 0.0).then_inc(s_set, 1)
            nc.gpsimd.memset(ones[:, :], 1.0).then_inc(s_set, 1)
            nc.gpsimd.memset(big[:, :], BIG).then_inc(s_set, 1)
            pool.wait_ge(s_set, SET_BIG)
            nc.gpsimd.memset(h3T[0][D:D + 1, :], 1.0).then_inc(s_set, 1)
            pool.wait_ge(s_set, SET_ROWS)
            for b in range(B):
                nc.gpsimd.memset(yg[b][:, :, :], 0.0).then_inc(s_set, 1)

            def scaled_l(b):
                c = col_sb[b]
                pool.wait_ge(s_cl, b + 1)
                nc.gpsimd.tensor_tensor(lb[b][:, :, :], hc[b][:, :, :], over(c[:, 20, :], D), ALU.mult).then_inc(s_lb, 1)
                nc.gpsimd.tensor_tensor(lbc[b][:, :, :], hc[b][:, :, :], over(c[:, 21, :], D), ALU.mult).then_inc(s_lb, 1)

            def scatter(b):
                if b == 0:
                    pool.wait_ge(d_zero, 16)
                pool.wait_ge(s_slot, b + 1)
                pool.wait_ge(s_h3, b + 1)
                for j in range(NT):
                    nc.gpsimd.indirect_dma_start(
                        slots_in[:, :], bass.IndirectOffsetOnAxis(ap=slot_i[b][:, j:j + 1], axis=0),
                        h3[b][:, j, :], None, bounds_check=SLOTS - 1, oob_is_err=False).then_inc(d_scatter, 16)

            def gather(b):
                for j in range(NT):
                    nc.gpsimd.indirect_dma_start(
                        yg[b][:, j, :], None, slots_out[:, :],
                        bass.IndirectOffsetOnAxis(ap=slot_i[b][:, j:j + 1], axis=0),
                        bounds_check=SLOTS - 1, oob_is_err=False).then_inc(d_gather[b][j // 4], 16)

            for b in range(B):
                scaled_l(b)
                scatter(b)
            pool.wait_ge(s_set, SET_YG)
            pool.wait_ge(d_yb, 16 * 2 * PAIRS)
            for b in range(B):
                gather(b)

        @block.scalar
        def _(act):
            def act_fn(out_ap, in_ap, fn, **kw):
                return nc.scalar.activation(out_ap, in_ap, fn, **kw)

            def mixing(b):
                for i in range(4):
                    act.wait_ge(s_proj, 5 * b + i + 1)
                    dst = (q_sb if i % 2 == 0 else k_sb)[b]
                    act_fn(dst[:, hs(i // 2)], S[(21 * b + i) % 3][:, :], ACT.Copy).then_inc(s_projev, 1)
                act.wait_ge(s_proj, 5 * b + 5)
                act_fn(v_sb[b][:, :, :].rearrange("p j d -> p (j d)"), S[(21 * b + 4) % 3][:, :], ACT.Copy).then_inc(s_projev, 1)

            def retained(b):
                act.wait_ge(s_gv, NT * (b + 1))
                act_fn(ret[b][:, :], R[:, :], ACT.Copy).then_inc(s_ret, 1)

            def root(b, k):
                c = col_sb[b]
                act.wait_ge(s_var[k], b + 1)
                act_fn(c[:, 30 + k, :], c[:, 25 + k, :], ACT.Sqrt).then_inc(s_root[k], 1)

            def recurrence(b):
                act.wait_ge(s_hc, b + 1)
                act_fn(sq[b][:, :, :], hc[b][:, :, :], ACT.Square).then_inc(s_hsq, 1)
                root(b, 0)
                for i in range(2):
                    act.wait_ge(s_vt, 2 * b + i + 1)
                    act_fn(vT[b][:, hs(i)], ABh[i][0:D, :], ACT.Copy).then_inc(s_vtev, 1)
                root(b, 1)
                for n, (i, c) in enumerate([(0, 0), (0, 1), (1, 0), (1, 1)]):
                    act.wait_ge(s_dx, 4 * b + n + 1)
                    act_fn(w[b][:, c, hs(i)], [M0[:, :], M3[:, :], ABh[0], ABh[1]][n], ACT.Relu).then_inc(s_u, 1)
                for g in range(4):
                    act.wait_ge(s_wt, 4 * b + g + 1)
                    tiles = 2 if g < 3 else 1
                    act_fn(wT[b][:, 2 * g:2 * g + tiles, :].rearrange("p j n -> p (j n)"),
                           ABh[g % 2][:, 0:tiles * 2 * P], ACT.Copy).then_inc(s_wtev, 1)
                act.wait_ge(s_a, b + 1)
                act_fn(aT[b][:, :], M0[:, :], ACT.Copy).then_inc(s_aev, 1)
                act_fn(aT2[b][:, :], M0[:, :], ACT.Square).then_inc(s_aev, 1)
                root(b, 2)
                act.wait_ge(s_q, b + 1)
                act.wait_ge(s_root[0], b + 1)
                act_fn(sq[b][:, :, :].rearrange("p j d -> p (j d)"), M3[:, :], ACT.Square).then_inc(s_qsq, 1)
                root(b, 3)
                act.wait_ge(s_h2, b + 1)
                act_fn(sq[b][:, :, :], h2c[b][:, :, :], ACT.Square).then_inc(s_h2sq, 1)
                root(b, 4)

            def routing(b):
                for i in range(2):
                    act.wait_ge(s_h3t, 2 * b + i + 1)
                    act_fn(h3T[b][0:D, hs(i)], ABh[i][0:D, :], ACT.Copy).then_inc(s_h3tev, 1)
                act.wait_ge(s_dl, b + 1)
                act_fn(ex[b][:, :, :], lg[b][:, :, :], ACT.Exp).then_inc(s_ex, 1)

            for b in range(B):
                mixing(b)
                retained(b)
                recurrence(b)
                routing(b)
            for p in range(PAIRS):
                act.wait_ge(s_xt, p + 1)
                act_fn(xbT[:, p, :, :, :].rearrange("d k g s -> d (k g s)"), AB[0:D, 0:2 * CAP], ACT.Copy).then_inc(s_xtev, 1)
                for g in range(2):
                    act.wait_ge(s_up, 4 * p + 2 * g + 1)
                    if p >= 2:
                        act.wait_ge(s_dn, p - 1)
                    e = p + PAIRS * g
                    a = PCOL["b1"][0] + 2 * e
                    act_fn(hm[:, p % 2, g, 0, :], S[0 if g == 0 else 2][:, 0:CAP], ACT.Relu,
                           bias=par[:, a:a + 1]).then_inc(s_hma, 1)

        @block.vector
        def _(dve):
            count = [0]

            def link(ins):
                count[0] += 1
                ins.then_inc(s_chain, 1)
                dve.wait_ge(s_chain, count[0])

            tt, tsc, stt = nc.vector.tensor_tensor, nc.vector.tensor_scalar, nc.vector.scalar_tensor_tensor

            def inverse_root(b, k, dst):
                c = col_sb[b]
                var, rt, r0, t = c[:, 25 + k, :], c[:, 30 + k, :], c[:, 35, :], c[:, 36, :]
                dve.wait_ge(s_root[k], b + 1)
                link(nc.vector.reciprocal(r0, rt))
                link(tt(t, r0, r0, ALU.mult))
                link(tt(t, t, var, ALU.mult))
                link(tsc(t, t, -0.5, 1.5, ALU.mult, ALU.add))
                link(tt(dst, r0, t, ALU.mult))

            def setup():
                dve.wait_ge(d_cst, 16)
                dve.wait_ge(d_par, 16)
                nc.vector.tensor_copy(tri_bf[:, :], ccol("tri")).then_inc(s_bfc, 1)
                nc.vector.memset(ones_bf[:, :], 1.0).then_inc(s_bfc, 1)
                et = pcol("et").rearrange("p (c d) -> p c d", c=2)
                link(nc.vector.tensor_reduce(et_mean[:, :], et, AX, ALU.add))
                link(tsc(et_mean[:, :], et_mean[:, :], 1.0 / D, None, ALU.mult))
                tt(etc[:, :, :], et, et_mean[:, :].unsqueeze(2).to_broadcast([P, 2, D]), ALU.subtract).then_inc(s_etc, 1)

            def mixing(b):
                for i in range(NT):
                    dve.wait_ge(d_gam[i], 16)
                    for f in range(2):
                        n = 2 * NT * b + 2 * i + f
                        dve.wait_ge(s_score, n + 1)
                        if n >= NG:
                            dve.wait_ge(s_gv, (n - NG) // 2 + 1)
                        tt(gs[:, n % NG, :], S[(21 * b + 5 + 2 * i + f) % 3][:, :], gam[:, i, hs(f)], ALU.mult).then_inc(s_gs, 1)

            def prelu_and_norm(b):
                c = col_sb[b]
                dve.wait_ge(s_mix, 2 * b + 2)
                dve.wait_ge(d_par, 16)
                bo = pcol("bo").unsqueeze(1).to_broadcast([P, NT, D])
                tt(y1[b][:, :, :], M0[:, :].rearrange("p (j d) -> p j d", d=D), bo, ALU.add).then_inc(s_y, 1)
                dve.wait_ge(s_y, b + 1)
                link(tsc(y2[b][:, :, :], y1[b][:, :, :], 0.0, pcol("a"), ALU.min, ALU.mult))
                link(stt(h[b][:, :, :], y1[b][:, :, :], 0.0, y2[b][:, :, :], ALU.max, ALU.add))
                link(nc.vector.tensor_reduce(c[:, 0, :], h[b][:, :, :], AX, ALU.add))
                link(tsc(c[:, 1, :], c[:, 0, :], 1.0 / D, None, ALU.mult))
                tt(hc[b][:, :, :], h[b][:, :, :], over(c[:, 1, :], D), ALU.subtract).then_inc(s_hc, 1)
                dve.wait_ge(s_hsq, b + 1)
                link(nc.vector.tensor_reduce(c[:, 2, :], sq[b][:, :, :], AX, ALU.add))
                tsc(c[:, 25, :], c[:, 2, :], 1.0 / D, LN_EPS, ALU.mult, ALU.add).then_inc(s_var[0], 1)
                link(tsc(c[:, 3, :], c[:, 2, :], 1.0 / D, None, ALU.mult))
                inverse_root(b, 0, c[:, 4, :])
                tt(vn[b][:, :, :], hc[b][:, :, :], over(c[:, 4, :], D), ALU.mult).then_inc(s_vn, 1)
                link(tt(c[:, 5, :], c[:, 4, :], c[:, 4, :], ALU.mult))
                link(tt(c[:, 5, :], c[:, 5, :], c[:, 3, :], ALU.mult))
                tsc(c[:, 26, :], c[:, 5, :], LN_EPS, None, ALU.add).then_inc(s_var[1], 1)
                dve.wait_ge(s_var[1], b + 1)
                inverse_root(b, 1, c[:, 6, :])
                link(tt(c[:, 7, :], c[:, 4, :], c[:, 6, :], ALU.mult))

            def normaliser(b):
                c = col_sb[b]
                U, M = M3[:, 0:NT], M3[:, NT:2 * NT]
                dve.wait_ge(s_usum, b + 1)
                tsc(c[:, 8, :], U, 1.0 / L1_EPS, 1.0, ALU.mult, ALU.min).then_inc(s_cm, 1)
                dve.wait_ge(s_m, b + 1)
                link(tsc(c[:, 9, :], M, 1.0, DECAY, ALU.min, ALU.mult))
                link(tt(c[:, 10, :], U, c[:, 9, :], ALU.add))
                link(tsc(c[:, 10, :], c[:, 10, :], L1_EPS, None, ALU.max))
                nc.vector.reciprocal(c[:, 11, :], c[:, 10, :]).then_inc(s_beta, 1)
                dve.wait_ge(s_beta, b + 1)
                link(stt(c[:, 20, :], c[:, 7, :], ccol("grow"), c[:, 11, :], ALU.mult, ALU.mult))
                tsc(c[:, 21, :], c[:, 20, :], TILE_DECAY, None, ALU.mult).then_inc(s_cl, 1)
                link(tsc(c[:, 12, :], c[:, 11, :], ccol("decay"), None, ALU.mult))

            def scans(b):
                dve.wait_ge(s_abc, b + 1)
                for n in range(2):
                    nc.vector.tensor_tensor_scan(w[b][:, n, 1:T], AB[:, 0:T - 1], w[b][:, n, 1:T], w[b][:, n, 0:1],
                                                 ALU.mult, ALU.add).then_inc(s_w, 1)

            def chunks(b):
                mask = ccol("upper").unsqueeze(1).to_broadcast([P, 4, P])
                for i in range(2):
                    dve.wait_ge(s_at, 2 * b + i + 1)
                    src = (M0 if i == 0 else M3)[:, :].rearrange("p (j t) -> p j t", t=P)
                    tt(att[b][:, 4 * i:4 * i + 4, :], src, mask, ALU.mult).then_inc(s_att, 1)
                for j in range(NT - 1):
                    dve.wait_ge(s_c, (NT - 1) * b + j + 1)
                    if j == 0:
                        nc.vector.tensor_copy(state[b][:, 1, :], M3[:, 0:2 * D]).then_inc(s_st, 1)
                    else:
                        stt(state[b][:, j + 1, :], state[b][:, j, :], TILE_DECAY, M3[:, 0:2 * D],
                            ALU.mult, ALU.add).then_inc(s_st, 1)
                    dve.wait_ge(s_st, (NT - 1) * b + j + 1)

            def outputs(b):
                c = col_sb[b]
                dve.wait_ge(s_sa, 2 * b + 2)
                link(tt(c[:, 13, :], c[:, 12, :], c[:, 12, :], ALU.mult))
                tt(c[:, 14, :], c[:, 13, :], M3[:, 0:NT], ALU.mult).then_inc(s_saev, 1)
                dve.wait_ge(s_saev, b + 1)
                tsc(c[:, 27, :], c[:, 14, :], 1.0 / D, LN_EPS, ALU.mult, ALU.add).then_inc(s_var[2], 1)
                for n, (i, k) in enumerate([(0, 0), (0, 1), (1, 0), (1, 1)]):
                    dve.wait_ge(s_dy, 4 * b + n + 1)
                    src = [ABh[0], ABh[1], M0[:, :], ABh[0]][n]
                    stt(yT[b][:, k, hs(i)], src, 0.0, w[b][:, k, hs(i)], ALU.max, ALU.mult).then_inc(s_yy, 1)
                inverse_root(b, 2, c[:, 15, :])
                link(tt(c[:, 16, :], c[:, 12, :], c[:, 15, :], ALU.mult))
                link(tt(c[:, 16, :], c[:, 16, :], c[:, 11, :], ALU.mult))
                link(tt(c[:, 17, :], c[:, 16, :], c[:, 16, :], ALU.mult))
                dve.wait_ge(s_qsq, b + 1)
                link(nc.vector.tensor_reduce(c[:, 18, :], sq[b][:, :, :], AX, ALU.add))
                link(tt(c[:, 18, :], c[:, 18, :], c[:, 17, :], ALU.mult))
                tsc(c[:, 28, :], c[:, 18, :], 1.0 / D, LN_EPS, ALU.mult, ALU.add).then_inc(s_var[3], 1)
                inverse_root(b, 3, c[:, 19, :])
                link(tt(c[:, 19, :], c[:, 19, :], c[:, 16, :], ALU.mult))
                tt(pq[b][:, :, :], M3[:, :].rearrange("p (j d) -> p j d", d=D), over(c[:, 19, :], D), ALU.mult).then_inc(s_p, 1)
                dve.wait_ge(s_p, b + 1)
                tt(h2c[b][:, :, :], hc[b][:, :, :], pq[b][:, :, :], ALU.add).then_inc(s_h2, 1)
                dve.wait_ge(s_h2sq, b + 1)
                link(nc.vector.tensor_reduce(c[:, 22, :], sq[b][:, :, :], AX, ALU.add))
                tsc(c[:, 29, :], c[:, 22, :], 1.0 / D, LN_EPS, ALU.mult, ALU.add).then_inc(s_var[4], 1)
                inverse_root(b, 4, c[:, 23, :])
                tt(h3[b][:, :, :], h2c[b][:, :, :], over(c[:, 23, :], D), ALU.mult).then_inc(s_h3, 1)

            def routing(b):
                c = col_sb[b]
                dve.wait_ge(s_lg, b + 1)
                Lp = M3[:, 0:NT * NE].rearrange("p (j e) -> p j e", e=NE)
                link(nc.vector.tensor_reduce(c[:, 24, :], Lp, AX, ALU.max))
                tt(lg[b][:, :, :], Lp, over(c[:, 24, :], NE), ALU.subtract).then_inc(s_dl, 1)
                dve.wait_ge(s_dl, b + 1)
                first = ccol("first").rearrange("p (j e) -> p j e", e=NE)
                base = ccol("base").rearrange("p (j e) -> p j e", e=NE)
                link(stt(key[b][:, :, :], lg[b][:, :, :], 0.0, first, ALU.is_equal, ALU.mult))
                link(nc.vector.tensor_reduce(c[:, 37, :], key[b][:, :, :], AX, ALU.max))
                tt(oh[b][:, :, :], key[b][:, :, :], over(c[:, 37, :], NE), ALU.is_equal).then_inc(s_oh, 1)
                dve.wait_ge(s_oh, b + 1)
                link(tt(key[b][:, :, :], oh[b][:, :, :], base, ALU.mult))
                link(nc.vector.tensor_reduce(c[:, 38, :], key[b][:, :, :], AX, ALU.add))
                dve.wait_ge(s_cum, b + 1)
                tt(key[b][:, :, :], M0[:, 0:NT * NE].rearrange("p (j e) -> p j e", e=NE), oh[b][:, :, :],
                   ALU.mult).then_inc(s_cumev, 1)
                dve.wait_ge(s_cumev, b + 1)
                link(nc.vector.tensor_reduce(c[:, 39, :], key[b][:, :, :], AX, ALU.add))
                link(stt(c[:, 38, :], c[:, 39, :], -1.0, c[:, 38, :], ALU.add, ALU.add))
                link(tsc(c[:, 39, :], c[:, 39, :], float(CAP), float(2 * SLOTS), ALU.is_gt, ALU.mult))
                tt(slot_i[b][:, :], c[:, 38, :], c[:, 39, :], ALU.add).then_inc(s_slot, 1)
                dve.wait_ge(s_ex, b + 1)
                link(nc.vector.tensor_reduce(c[:, 0, :], ex[b][:, :, :], AX, ALU.add))
                link(nc.vector.reciprocal(c[:, 2, :], c[:, 0, :]))

            def experts(p):
                for g in range(2):
                    dve.wait_ge(s_up, 4 * p + 2 * g + 2)
                    if p >= 2:
                        dve.wait_ge(s_dn, p - 1)
                    a = PCOL["b1"][0] + 2 * (p + PAIRS * g) + 1
                    tsc(hm[:, p % 2, g, 1, :], (S[1] if g == 0 else M0)[:, 0:CAP], par[:, a:a + 1], 0.0,
                        ALU.add, ALU.max).then_inc(s_hmd, 1)
                dve.wait_ge(s_dn, p + 1)
                a = PCOL["b2"][0] + p * D
                b2 = par[:, a:a + D].unsqueeze(1).to_broadcast([P, KS, D])
                src = (R if p % 2 == 0 else M3)[:, 0:CAP].rearrange("p (k d) -> p k d", d=D)
                tt(yb_sb[:, p, :, :], src, b2, ALU.add).then_inc(s_yb, 1)

            def finish(b, g):
                c = col_sb[b]
                t4 = slice(4 * g, 4 * g + 4)
                y, pos, mask, rep = yg[b][:, t4, :], fpos[:, :, :], fmask[:, :, :], frep[:, :, :]
                z = fin[b][:, t4, :]

                def ov(col):
                    return col.unsqueeze(2).to_broadcast([P, 4, D])
                dve.wait_ge(d_gather[b][g], 16 * 4)
                link(tt(y, y, ov(c[:, 2, t4]), ALU.mult))
                link(tsc(pos, y, 0.0, None, ALU.max))
                link(stt(y, y, 0.0, pos, ALU.min, ALU.add))
                tsc(rep, y, 1e4, -1e4, ALU.min, ALU.max)
                link(tsc(mask, y, 0.0, 0.0, ALU.mult, ALU.is_equal))
                link(nc.vector.copy_predicated(rep, mask, y))
                link(tt(z, h2c[b][:, t4, :], ov(c[:, 1, t4]), ALU.add))
                tt(z, z, rep, ALU.add).then_inc(s_fin, 1)

            for b in range(B):
                mixing(b)
                if b == 0:
                    setup()
                prelu_and_norm(b)
                normaliser(b)
                scans(b)
                chunks(b)
                outputs(b)
                routing(b)
            for p in range(PAIRS):
                experts(p)
            for b in range(B):
                for g in range(2):
                    finish(b, g)

        @block.tensor
        def _(pe):
            mm = nc.tensor.matmul

            def mixing(b):
                pe.wait_ge(d_wa, 16)
                pe.wait_ge(d_x[b], 16)

                def bank_free(n):
                    m = n - 3
                    if m < 0:
                        return
                    mb, i = divmod(m, 21)
                    if i < 5:
                        pe.wait_ge(s_projev, 5 * mb + i + 1)
                    else:
                        pe.wait_ge(s_gs, 16 * mb + i - 5 + 1)

                for i in range(4):
                    n = 21 * b + i
                    bank_free(n)
                    mm(S[n % 3][:, :], wa_sb[:, (i % 2) * P:(i % 2 + 1) * P], x_sb[b][:, hs(i // 2)],
                       start=True, stop=True).then_inc(s_proj, 1)
                n = 21 * b + 4
                bank_free(n)
                for j in range(NT):
                    last = mm(S[n % 3][:, j * D:(j + 1) * D], x_sb[b][:, ts(j)], wa_sb[:, 4 * D:5 * D], start=True, stop=True)
                last.then_inc(s_proj, 1)

                def retained_part(i):
                    pe.wait_ge(s_gs, 16 * b + 2 * i + 2)
                    for f in range(2):
                        last = mm(R[D * f:D * f + D, :], v_sb[b][:, i, :], gs[:, (16 * b + 2 * i + f) % NG, :],
                                  start=(i == 0), stop=(i == NT - 1))
                    last.then_inc(s_gv, 1)

                pe.wait_ge(s_projev, 5 * b + 5)
                if b > 0:
                    pe.wait_ge(s_ret, b)
                for i in range(NT):
                    for f in range(2):
                        n = 21 * b + 5 + 2 * i + f
                        bank_free(n)
                        r = 64 * f
                        mm(S[n % 3][:, :], k_sb[b][r:r + 64, ts(i)], q_sb[b][r:r + 64, hs(f)],
                           start=True, stop=True).then_inc(s_score, 1)
                    if i >= 1:
                        retained_part(i - 1)
                retained_part(NT - 1)

            def recurrence(b):
                pe.wait_ge(s_ret, b + 1)
                pe.wait_ge(d_par, 16)
                if b > 0:
                    pe.wait_ge(s_cumev, b)
                for f in range(2):
                    if f == 1:
                        pe.wait_ge(s_mix, 2 * b + 1)
                    for j in range(4 * f, 4 * f + 4):
                        last = mm(M0[:, j * D:(j + 1) * D], ret[b][64 * f:64 * f + 64, ts(j % 4)], pcol("wo", 64 * f, 64 * f + 64),
                                  start=True, stop=True)
                    last.then_inc(s_mix, 1)
                pe.wait_ge(d_cst, 16)
                pe.wait_ge(s_vn, b + 1)
                if b > 0:
                    pe.wait_ge(s_h3tev, 2 * b)
                for i in range(2):
                    for j in range(4):
                        last = nc.tensor.transpose(ABh[i][0:D, ts(j)], vn[b][:, 4 * i + j, :], ccol("ident"))
                    last.then_inc(s_vt, 1)
                for n, (i, c) in enumerate([(0, 0), (0, 1), (1, 0), (1, 1)]):
                    pe.wait_ge(s_vtev, 2 * b + i + 1)
                    if n == 0:
                        pe.wait_ge(s_y, b + 1)
                    if n == 1 and b > 0:
                        pe.wait_ge(s_dl, b)
                    if n == 2:
                        pe.wait_ge(s_vtev, 2 * b + 2)
                    a = PCOL["dxt"][0] + c * P
                    mm([M0[:, :], M3[:, :], ABh[0], ABh[1]][n], par[0:D, a:a + P], vT[b][:, hs(i)],
                       start=True, stop=True).then_inc(s_dx, 1)
                pe.wait_ge(s_set, SET_BIG)
                pe.wait_ge(s_u, 4 * b + 4)
                for j in range(NT):
                    for c in range(2):
                        last = mm(M3[:, j:j + 1], w[b][:, c, ts(j)], ones[:, :], start=(c == 0), stop=(c == 1))
                last.then_inc(s_usum, 1)
                pe.wait_ge(s_cm, b + 1)
                cm = col_sb[b][:, 8, :]
                mm(M3[:, NT:2 * NT], ccol("near"), cm, start=True, stop=False)
                mm(M3[:, NT + 1:2 * NT], ccol("prev"), cm[:, 0:NT - 1], start=False, stop=False)
                for d in range(2, NT):
                    last = mm(M3[:, NT + d:2 * NT], big[:, :], cm[:, 0:NT - d], start=False, stop=(d == NT - 1))
                last.then_inc(s_m, 1)
                pe.wait_ge(s_beta, b + 1)
                for j in range(NT):
                    last = mm(ABh[j // 4][:, ts(j % 4)], col_sb[b][:, 11, j:j + 1].to_broadcast([P, P]), ccol("ident97"),
                              start=True, stop=True)
                last.then_inc(s_abc, 1)

                pe.wait_ge(s_w, 2 * b + 2)
                for j in range(NT):
                    for c in range(2):
                        last = mm((M0 if j < 4 else M3)[:, ts(j % 4)], w[b][:, c, ts(j)], w[b][:, c, ts(j)],
                                  start=(c == 0), stop=(c == 1))
                    if j % 4 == 3:
                        last.then_inc(s_at, 1)

                def turned(g):
                    if g >= 2:
                        pe.wait_ge(s_wtev, 4 * b + g - 1)
                    for j in range(2 * g, min(2 * g + 2, NT - 1)):
                        for c in range(2):
                            at = (j % 2) * 2 * P + c * P
                            last = nc.tensor.transpose(ABh[g % 2][:, at:at + P], w[b][:, c, ts(j)], ccol("ident"))
                    last.then_inc(s_wt, 1)

                turned(0)
                turned(1)
                pe.wait_ge(s_lb, 2 * b + 2)
                pe.wait_ge(s_att, 2 * b + 2)
                for j in range(NT):
                    if j < NT - 1:
                        if j in (2, 4):
                            turned(j // 2 + 1)
                        pe.wait_ge(s_wtev, 4 * b + j // 2 + 1)
                        if j > 0:
                            pe.wait_ge(s_st, (NT - 1) * b + j)
                        for c in range(2):
                            last = mm(M3[:, c * D:(c + 1) * D], wT[b][:, j, ts(c)], lbc[b][:, j, :], start=True, stop=True)
                        last.then_inc(s_c, 1)
                    f = j // 4
                    dst = M0[D * f:D * f + D, ts(j % 4)]
                    last = mm(dst, lb[b][:, j, :], att[b][:, j, :], start=True, stop=(j == 0))
                    if j > 0:
                        pe.wait_ge(s_st, (NT - 1) * b + j)
                        for c in range(2):
                            last = mm(dst, state[b][:, j, c * D:(c + 1) * D], w[b][:, c, ts(j)], start=False, stop=(c == 1))
                last.then_inc(s_a, 1)
                pe.wait_ge(s_aev, 2 * b + 2)
                pe.wait_ge(s_st, (NT - 1) * (b + 1))
                for f in range(2):
                    if f == 1:
                        pe.wait_ge(s_sa, 2 * b + 1)
                    for j in range(4 * f, 4 * f + 4):
                        last = mm(M3[:, j:j + 1], aT2[b][64 * f:64 * f + 64, ts(j % 4)], ones[64 * f:64 * f + 64, :],
                                  start=True, stop=True)
                    last.then_inc(s_sa, 1)
                pe.wait_ge(s_wtev, 4 * b + 4)
                for n, (i, c) in enumerate([(0, 0), (0, 1), (1, 0), (1, 1)]):
                    if n == 3:
                        pe.wait_ge(s_yy, 4 * b + 1)
                    a = PCOL["dyt"][0] + c * P
                    mm([ABh[0], ABh[1], M0[:, :], ABh[0]][n], par[64 * i:64 * i + 64, a:a + P], aT[b][64 * i:64 * i + 64, :],
                       start=True, stop=True).then_inc(s_dy, 1)
                pe.wait_ge(s_etc, 1)
                pe.wait_ge(s_saev, b + 1)
                pe.wait_ge(s_yy, 4 * b + 4)
                for j in range(NT):
                    for c in range(2):
                        last = mm(M3[:, j * D:(j + 1) * D], yT[b][:, c, ts(j)], etc[:, c, :], start=(c == 0), stop=(c == 1))
                last.then_inc(s_q, 1)

            def routing(b):
                pe.wait_ge(s_h3, b + 1)
                for i in range(2):
                    for j in range(4):
                        last = nc.tensor.transpose(ABh[i][0:D, ts(j)], h3[b][:, 4 * i + j, :], ccol("ident"))
                    last.then_inc(s_h3t, 1)
                pe.wait_ge(s_h3tev, 2 * b + 2)
                pe.wait_ge(d_gate, 16)
                pe.wait_ge(s_set, SET_ROWS)
                pe.wait_ge(s_p, b + 1)
                for j in range(NT):
                    last = mm(M3[:, j * NE:(j + 1) * NE], h3T[b][:, ts(j)], gate_sb[:, :], start=True, stop=True)
                last.then_inc(s_lg, 1)
                pe.wait_ge(s_bfc, 2)
                pe.wait_ge(s_oh, b + 1)
                terms = [(M0[:, 0:NT * NE], tri_bf, oh[b][:, :, :].rearrange("p j e -> p (j e)"))]
                for d in range(1, NT):
                    terms.append((M0[:, d * NE:NT * NE], ones_bf, oh[b][:, 0:NT - d, :].rearrange("p j e -> p (j e)")))
                for a in range(b):
                    for i in range(NT):
                        terms.append((M0[:, 0:NT * NE].rearrange("p (j e) -> p j e", e=NE), ones_bf,
                                      oh[a][:, i:i + 1, :].to_broadcast([P, NT, NE])))
                for n, (dst, lhs, rhs) in enumerate(terms):
                    last = mm(dst, lhs[:, :], rhs, start=(n == 0), stop=(n == len(terms) - 1))
                last.then_inc(s_cum, 1)

            for b in range(B):
                mixing(b)
                recurrence(b)
                routing(b)

            def slots_turned(p):
                pe.wait_ge(d_xb[p], 32)
                if p >= 1:
                    pe.wait_ge(s_xtev, p)
                for k in range(KS):
                    last = nc.tensor.transpose(AB[0:D, k * P:(k + 1) * P], xb[:, p, k, :], ccol("ident"))
                last.then_inc(s_xt, 1)

            pe.wait_ge(s_h3tev, 2 * B)
            pe.wait_ge(s_cumev, B)
            pe.wait_ge(s_dl, B)
            pe.wait_ge(s_gs, 16 * B)
            pe.wait_ge(s_ret, B)
            pe.wait_ge(d_w1, 16)
            pe.wait_ge(d_w2, 16)
            slots_turned(0)
            for p in range(PAIRS):
                pe.wait_ge(s_xtev, p + 1)
                for g in range(2):
                    for c in range(2):
                        if p > 0:
                            pe.wait_ge(s_hma if c == 0 else s_hmd, 2 * (p - 1) + g + 1)
                        dst = (S[2 * g] if c == 0 else (S[1] if g == 0 else M0))[:, 0:CAP]
                        mm(dst, w1_sb[:, p + PAIRS * g, ts(c)], xbT[:, p, :, g, :], start=True, stop=True).then_inc(s_up, 1)
                if p + 1 < PAIRS:
                    slots_turned(p + 1)
                pe.wait_ge(s_hma, 2 * p + 2)
                pe.wait_ge(s_hmd, 2 * p + 2)
                if p >= 2:
                    pe.wait_ge(s_yb, p - 1)
                bank = R if p % 2 == 0 else M3
                for k in range(KS):
                    for c in range(2):
                        for g in range(2):
                            last = mm(bank[64 * g:64 * g + 64, k * D:(k + 1) * D], hm[:, p % 2, g, c, k * D:(k + 1) * D],
                                      w2_sb[:, p + PAIRS * g, c, :], start=(c == 0), stop=(c == 1))
                last.then_inc(s_dn, 1)


def constants(np):
    out = np.zeros((P, CWIDTH), np.float32)

    def put(name, value):
        out[:, CCOL[name][0]:CCOL[name][1]] = value
    s, t = np.arange(P)[:, None], np.arange(P)[None, :]
    put("ident", (s == t))
    put("ident97", DECAY * (s == t))
    put("upper", (s < t))
    put("tri", (s <= t))

    def power(k):
        return np.where(k >= 3, BIG, (DECAY / L1_EPS) ** np.clip(k, 0, 2).astype(np.float64))
    put("near", np.where(s < t, power(t - 1 - s), 0.0))
    put("prev", power(t - 1 - s + P))
    put("grow", DECAY ** -(s + 1.0))
    put("decay", DECAY ** (s * 1.0))
    e = np.arange(NT * NE)[None, :] % NE
    put("first", (NE - e) * np.ones((P, 1)))
    put("base", (CAP * e) * np.ones((P, 1)))
    return out


def kernel(**inputs):
    import numpy as np
    import concourse.bacc as bacc
    from concourse.bass_utils import run_bass_kernel_spmd

    g = {k: np.asarray(v) for k, v in inputs.items()}
    f = np.float32
    x = g["x"].reshape(B, T, D)
    xT = np.concatenate([x.transpose(0, 2, 1), np.ones((B, 1, T), f)], axis=1)
    rows = lambda w, b: np.concatenate([g[w], g[b][None, :]], axis=0)
    q, k, v = rows("L0_tok_Wq", "L0_tok_bq"), rows("L0_tok_Wk", "L0_tok_bk"), rows("L0_tok_Wv", "L0_tok_bv")
    wa = np.concatenate([q, q, k, k, v], axis=1)
    gammaT = g["L0_tok_d_gamma_batched"].T.reshape(NT, P, T)
    params = np.zeros((P, PWIDTH), f)

    def put(name, value, hi=P):
        params[0:hi, PCOL[name][0]:PCOL[name][1]] = value
    put("wo", np.concatenate([g["L0_tok_Wo"]] * 2, axis=0))
    put("bo", g["L0_tok_bo"][None, :])
    put("dxt", g["L0_attn_Dx"].T, D)
    put("dyt", np.concatenate([g["L0_attn_Dy"].T] * 2, axis=0))
    put("et", g["L0_attn_E"].T.reshape(2, P, D).transpose(1, 0, 2).reshape(P, 2 * D))
    put("a", g["L0_tok_prelu_a"].reshape(1, 1))
    put("b1", g["L0_ffn_b1"].reshape(NE * 2, P).T)
    b2 = g["L0_ffn_b2"].reshape(2, 1, PAIRS * D)
    put("b2", np.broadcast_to(b2, (2, 64, PAIRS * D)).reshape(P, PAIRS * D))
    gate = np.concatenate([g["L0_ffn_gate_w"], g["L0_ffn_gate_b"][None, :]], axis=0)
    arrays = {"xT": xT, "wa": wa, "gammaT": gammaT, "params": params, "consts": constants(np), "gate": gate,
              "w1": g["L0_ffn_w1"], "w2": g["L0_ffn_w2"]}
    arrays = {n: np.ascontiguousarray(a, dtype=f) for n, a in arrays.items()}

    nc = bacc.Bacc("TRN2", target_bir_lowering=False, num_devices=1)
    f32 = mybir.dt.float32
    aps = {n: nc.dram_tensor(n, a.shape, f32, kind="ExternalInput").ap() for n, a in arrays.items()}
    out = nc.dram_tensor("out", (B, T, D), f32, kind="ExternalOutput").ap()
    slots_in = nc.dram_tensor("slots_in", (SLOTS, D), f32, kind="Internal").ap()
    slots_out = nc.dram_tensor("slots_out", (SLOTS, D), f32, kind="Internal").ap()
    build(nc, out=out, slots_in=slots_in, slots_out=slots_out, **aps)
    r = run_bass_kernel_spmd(nc, [arrays], core_ids=[0])
    return r.results[0]["out"]
```

```python
import concourse.bass as bass
from concourse import mybir
from contextlib import ExitStack

B, T, D = 2, 1024, 64
N = 256
NE, F = 8, 256
P = 128
NT = T // P
HALF = T // 2
CAP = (5 * B * T) // (4 * NE)
SLOTS = NE * CAP
KS = CAP // 64
PAIRS = NE // 2
DECAY = 0.97
TILE_DECAY = DECAY ** P
WARM = 6
LN_EPS, L1_EPS = 1e-5, 1e-12
BIG = 1e35

PARAMS = [("wo", 2 * D), ("bo", D), ("dxt", N), ("dyt", N), ("et", 2 * D), ("a", 1), ("b1", 2 * NE), ("b2", PAIRS * D), ("gate", 2 * NE), ("gb", NE)]
CONSTS = [("ident", P), ("ident97", P), ("upper", P), ("tri", P), ("near", P), ("prev", P),
          ("grow", 1), ("decay", 1), ("first", NT * NE), ("base", NT * NE), ("halves", 2)]


def place(tau):
    return 2 * (tau % 4) + tau // 4


GROUPS = [(0, 0, 4), (0, 4, 4), (1, 0, 4), (1, 4, 2), (1, 6, 2)]


def program_order():
    def mixing(b):
        out = [("proj", b, i) for i in range(5)]
        out += [("score", b, i) for i in range(2 * NT)]
        return out + [("retained", b, 0)]

    def recurrence(b):
        return ([("wo", b, 0), ("prelu", b, 0), 2, ("centre", b, 0), 2, ("norm", b, 0), 2, ("norm", b, 1), 1, ("vt", b, 0), 1]
                + [("dx", b, n) for n in range(4)] + [1, ("usum", b, 0), 1, ("clamp", b, 0), 1, ("beta", b, 0), 1]
                + [("scan", b, 0), ("at", b, 0), ("scan", b, 1), ("at", b, 1), ("wt", b, 0), ("wt", b, 1)]
                + sum([[("chunk", b, j)] + [1] * (j % 2) for j in range(NT)], [])
                + [("aT", b, 0), 1] + [("dy", b, n) for n in range(4)] + [1, ("q", b, 0), 1, ("q", b, 1), 2, ("h2", b, 0), 2]
                + [("h3", b, 0), 1, ("gate", b, 0), 1, ("slots", b, 0)])

    order = mixing(0)
    fill = mixing(1)
    for stage in recurrence(0):
        if isinstance(stage, int):
            order, fill = order + fill[:stage], fill[stage:]
        else:
            order.append(stage)
    return order + fill + [stage for stage in recurrence(1) if not isinstance(stage, int)]


ORDER = program_order()


def columns(table):
    at, out = 0, {}
    for name, width in table:
        out[name] = (at, at + width)
        at += width
    return out, at


PCOL, PWIDTH = columns(PARAMS)
CCOL, CWIDTH = columns(CONSTS)


def build(nc, xT, wa, gammaT, params, consts, w1, w2, out, slots_in, slots_out):
    f32, bf16, i32 = mybir.dt.float32, mybir.dt.bfloat16, mybir.dt.int32
    ALU = mybir.AluOpType
    ACT = mybir.ActivationFunctionType
    AX = mybir.AxisListType.X

    ctx = ExitStack()
    with ctx:
        def sb(name, shape, dt=f32):
            return ctx.enter_context(nc.sbuf_tensor(name, shape, dt))

        def pb(name, shape, dt=f32):
            return ctx.enter_context(nc.psum_tensor(name, shape, dt))

        def sem(name):
            return ctx.enter_context(nc.semaphore(name))

        def both(name, shape, dt=f32):
            return [sb(f"{name}_{b}", shape, dt) for b in range(B)]

        def shared(name, shape, dt=f32):
            return [sb(name, shape, dt)] * B

        x_sb = both("x_sb", [D + 1, T])
        wa_sb = sb("wa_sb", [D + 1, 5 * D])
        gam = sb("gam", [P, NT, T])
        par = sb("par", [P, PWIDTH])
        cst = sb("cst", [P, CWIDTH])
        warm = sb("warm", [P, HALF], bf16)
        w1_sb = sb("w1_sb", [D, NE, F])
        w2_sb = sb("w2_sb", [P, NE, 2, D])
        ones = sb("ones", [P, 1])
        ones8 = sb("ones8", [P, NT])
        junk = sb("junk", [P, 1])
        big = sb("big", [P, P])
        zeros = sb("zeros", [P, SLOTS * D // P])
        tri_bf = sb("tri_bf", [P, P], bf16)
        ones_bf = sb("ones_bf", [P, P], bf16)
        etc = sb("etc", [P, 2, D])
        et_mean = sb("et_mean", [P, 2])

        q_sb = shared("q_sb", [P, T])
        k_sb = shared("k_sb", [P, T])
        v_sb = shared("v_sb", [P, NT, D])
        NG = 6
        gs = sb("gs", [P, NG, HALF])
        ret = shared("ret", [P, HALF])
        y1 = shared("y1", [P, NT, D])
        y2 = shared("y2", [P, NT, D])
        h = shared("h", [P, NT, D])
        hc = shared("hc", [P, NT, D])
        sq = shared("sq", [P, NT, D])
        vn = shared("vn", [P, NT, D])
        lb = shared("lb", [P, NT, D])
        lbc = shared("lbc", [P, NT, D])
        vT = shared("vT", [P, HALF])
        w = shared("w_all", [P, 2, T])
        wT = shared("wT", [P, NT, 2 * P])
        att = shared("att", [P, NT, P])
        state = shared("state", [P, NT, 2 * D])
        aT = shared("aT", [P, HALF])
        aT2 = shared("aT2", [P, HALF])
        yT = shared("yT", [P, 2, T])
        pq = shared("pq", [P, NT, D])
        h2c = both("h2c", [P, NT, D])
        h3 = both("h3", [P, NT, D])
        h3T = shared("h3T", [P, HALF])
        lg = both("lg", [P, NT, NE])
        ex = both("ex", [P, NT, NE])
        key = both("key", [P, NT, NE])
        oh = both("oh", [P, NT, NE], bf16)
        slot_i = both("slot_i", [P, NT], i32)
        yg = both("yg", [P, NT, D])
        NC = 40
        col_sb = both("col_sb", [P, NC, NT])
        xb = sb("xb", [P, PAIRS, KS, D])
        xbT = sb("xbT", [D, PAIRS, KS, 2, D])
        hm = sb("hm", [P, 2, 2, 2, CAP])
        yb_sb = sb("yb_sb", [P, PAIRS, KS, D])
        fin = both("fin", [P, NT, D])
        fpos = sb("fpos", [P, 4, D])
        fmask = sb("fmask", [P, 4, D], i32)
        frep = sb("frep", [P, 4, D])

        S = [pb(f"S{i}", [P, HALF]) for i in range(3)]
        R = pb("R", [P, HALF])
        M0 = pb("M0", [P, HALF])
        M3 = pb("M3", [P, HALF])
        AB = pb("AB", [P, T])
        ABh = [AB[:, 0:HALF], AB[:, HALF:T]]

        def pcol(name, lo=0, hi=P):
            a, z = PCOL[name]
            return par[lo:hi, a:z]

        def ccol(name):
            a, z = CCOL[name]
            return cst[:, a:z]

        DXB = [M0[:, :], M3[:, :], ABh[0], ABh[1]]
        DYB = [ABh[0], ABh[1], M0[:, :], ABh[0]]
        UPB = [S[0], S[1], S[2], M0]

        def ts(j):
            return slice(j * P, (j + 1) * P)

        def hs(i):
            return slice(i * HALF, (i + 1) * HALF)

        def over(col, n):
            return col.unsqueeze(2).to_broadcast([P, NT, n])

        d_x = [sem(f"d_x{b}") for b in range(B)]
        d_wa, d_par, d_cst, d_w1, d_w2 = (sem(n) for n in ("d_wa", "d_par", "d_cst", "d_w1", "d_w2"))
        d_gam = [sem(f"d_gam{i}") for i in range(NT)]
        d_zero, d_scatter, d_out = sem("d_zero"), sem("d_scatter"), sem("d_out")
        d_xb = [sem(f"d_xb{p}") for p in range(PAIRS)]
        d_yb = sem("d_yb")
        d_gather = [sem(f"d_gather{g}") for g in range(len(GROUPS))]
        s_set = sem("s_set")
        s_bfc = sem("s_bfc")
        s_etc = sem("s_etc")
        s_proj, s_projev = sem("s_proj"), sem("s_projev")
        s_score, s_gs, s_gv = sem("s_score"), sem("s_gs"), sem("s_gv")
        s_ret, s_mix, s_y = sem("s_ret"), sem("s_mix"), sem("s_y")
        s_hc, s_hsq = sem("s_hc"), sem("s_hsq")
        s_var = [sem(f"s_var{k}") for k in range(5)]
        s_root = [sem(f"s_root{k}") for k in range(5)]
        s_vn, s_vt, s_vtev = sem("s_vn"), sem("s_vt"), sem("s_vtev")
        s_dx, s_u = sem("s_dx"), sem("s_u")
        s_usum, s_cm, s_m, s_beta = sem("s_usum"), sem("s_cm"), sem("s_m"), sem("s_beta")
        s_abc, s_w = sem("s_abc"), sem("s_w")
        s_cl, s_lb = sem("s_cl"), sem("s_lb")
        s_at, s_att = sem("s_at"), sem("s_att")
        s_wt, s_wtev = sem("s_wt"), sem("s_wtev")
        s_c, s_st = sem("s_c"), sem("s_st")
        s_a, s_aev = sem("s_a"), sem("s_aev")
        s_sa, s_saev = sem("s_sa"), sem("s_saev")
        s_dy, s_yy = sem("s_dy"), sem("s_yy")
        s_q, s_qsq, s_p = sem("s_q"), sem("s_qsq"), sem("s_p")
        s_h2, s_h2sq, s_h3 = sem("s_h2"), sem("s_h2sq"), sem("s_h3")
        s_h3t, s_h3tev = sem("s_h3t"), sem("s_h3tev")
        s_lg, s_lgev, s_dl, s_ex = sem("s_lg"), sem("s_lgev"), sem("s_dl"), sem("s_ex")
        s_oh, s_cum, s_cumev, s_slot = sem("s_oh"), sem("s_cum"), sem("s_cumev"), sem("s_slot")
        s_xt, s_xtev = sem("s_xt"), sem("s_xtev")
        s_up, s_hma, s_hmd = sem("s_up"), sem("s_hma"), sem("s_hmd")
        s_dn, s_yb = sem("s_dn"), sem("s_yb")
        s_fin = sem("s_fin")
        s_chain = sem("s_chain")
        s_pchain = sem("s_pchain")

        SET_WARM, SET_ZERO, SET_BIG, SET_YG = 1, 2, 4, 6
        block = ctx.enter_context(nc.Block())

        @block.sync
        def _(sp):
            sp.dma_start(wa_sb[:, :], wa).then_inc(d_wa, 16)
            sp.dma_start(x_sb[0][:, :], xT[0]).then_inc(d_x[0], 16)
            for i in range(NT):
                sp.dma_start(gam[:, i, :], gammaT[i]).then_inc(d_gam[i], 16)
            sp.dma_start(par[:, :], params).then_inc(d_par, 16)
            sp.dma_start(x_sb[1][:, :], xT[1]).then_inc(d_x[1], 16)
            sp.dma_start(cst[:, :], consts).then_inc(d_cst, 16)
            sp.dma_start(w1_sb[:, :, :], w1.rearrange("e d f -> d e f")).then_inc(d_w1, 16)
            sp.dma_start(w2_sb[:, :, :, :], w2.rearrange("e (c p) d -> p e c d", c=2)).then_inc(d_w2, 16)
            sp.wait_ge(s_set, SET_ZERO)
            sp.dma_start(slots_in.rearrange("(p r) d -> p (r d)", p=P), zeros[:, :]).then_inc(d_zero, 16)
            sp.wait_ge(d_scatter, 16 * B * NT)
            src = slots_in.rearrange("(g e p k) d -> g e p (k d)", g=2, e=PAIRS, p=64)
            for p in range(PAIRS):
                for g in range(2):
                    sp.dma_start(xb[64 * g:64 * g + 64, p, :, :].rearrange("p k d -> p (k d)"), src[g, p]).then_inc(d_xb[p], 16)
            dst = slots_out.rearrange("(g e p k) d -> g e p (k d)", g=2, e=PAIRS, p=64)
            for p in range(PAIRS):
                sp.wait_ge(s_yb, p + 1)
                for g in range(2):
                    sp.dma_start(dst[g, p], yb_sb[64 * g:64 * g + 64, p, :, :].rearrange("p k d -> p (k d)")).then_inc(d_yb, 16)
            for n, (b, first, tiles) in enumerate(GROUPS):
                sp.wait_ge(s_fin, n + 1)
                for f in range(2):
                    lo, hi = f * HALF + first // 2 * P, f * HALF + (first + tiles) // 2 * P
                    sp.dma_start(out[b, lo:hi, :].rearrange("(j p) d -> p j d", p=P),
                                 fin[b][:, first + f:first + tiles:2, :]).then_inc(d_out, 16)
            sp.wait_ge(d_out, 16 * 2 * len(GROUPS))

        @block.gpsimd
        def _(pool):
            nc.gpsimd.memset(warm[:, :], 0.0).then_inc(s_set, 1)
            nc.gpsimd.memset(zeros[:, :], 0.0).then_inc(s_set, 1)
            nc.gpsimd.memset(ones[:, :], 1.0).then_inc(s_set, 1)
            nc.gpsimd.memset(big[:, :], BIG).then_inc(s_set, 1)
            for b in range(B):
                nc.gpsimd.memset(yg[b][:, :, :], 0.0).then_inc(s_set, 1)

            def scaled_l(b):
                c = col_sb[b]
                pool.wait_ge(s_cl, b + 1)
                nc.gpsimd.tensor_tensor(lbc[b][:, :, :], hc[b][:, :, :], over(c[:, 21, :], D), ALU.mult).then_inc(s_lb, 1)
                nc.gpsimd.tensor_tensor(lb[b][:, :, :], hc[b][:, :, :], over(c[:, 20, :], D), ALU.mult).then_inc(s_lb, 1)

            def scatter(b):
                if b == 0:
                    pool.wait_ge(d_zero, 16)
                pool.wait_ge(s_slot, b + 1)
                pool.wait_ge(s_h3, b + 1)
                for j in range(NT):
                    nc.gpsimd.indirect_dma_start(
                        slots_in[:, :], bass.IndirectOffsetOnAxis(ap=slot_i[b][:, j:j + 1], axis=0),
                        h3[b][:, j, :], None, bounds_check=SLOTS - 1, oob_is_err=False).then_inc(d_scatter, 16)

            for b in range(B):
                scaled_l(b)
                scatter(b)
            pool.wait_ge(s_set, SET_YG)
            pool.wait_ge(d_yb, 16 * 2 * PAIRS)
            for n, (b, first, tiles) in enumerate(GROUPS):
                for j in range(first, first + tiles):
                    nc.gpsimd.indirect_dma_start(
                        yg[b][:, j, :], None, slots_out[:, :],
                        bass.IndirectOffsetOnAxis(ap=slot_i[b][:, j:j + 1], axis=0),
                        bounds_check=SLOTS - 1, oob_is_err=False).then_inc(d_gather[n], 16)

        @block.scalar
        def _(act):
            fn = nc.scalar.activation

            def proj(b, i):
                act.wait_ge(s_proj, 5 * b + i + 1)
                dst = [q_sb[b][:, hs(0)], k_sb[b][:, hs(0)], q_sb[b][:, hs(1)], k_sb[b][:, hs(1)],
                       v_sb[b][:, :, :].rearrange("p j d -> p (j d)")][i]
                fn(dst, S[(21 * b + i) % 3][:, :], ACT.Copy).then_inc(s_projev, 1)

            def retained(b, i):
                act.wait_ge(s_gv, NT * (b + 1))
                fn(ret[b][:, :], R[:, :], ACT.Copy).then_inc(s_ret, 1)

            def half_root(b, k):
                c = col_sb[b]
                act.wait_ge(s_var[k], b + 1)
                fn(c[:, 30 + k, :], c[:, 25 + k, :], ACT.Sqrt, scale=0.25).then_inc(s_root[k], 1)

            def centre(b, i):
                act.wait_ge(s_hc, b + 1)
                fn(sq[b][:, :, :], hc[b][:, :, :], ACT.Square).then_inc(s_hsq, 1)

            def norm(b, k):
                half_root(b, k)

            def vt(b, i):
                act.wait_ge(s_vt, b + 1)
                fn(vT[b][:, :], ABh[0], ACT.Copy).then_inc(s_vtev, 1)

            def dx(b, n):
                act.wait_ge(s_dx, 4 * b + n + 1)
                fn(w[b][:, n // 2, hs(n % 2)], DXB[n], ACT.Relu).then_inc(s_u, 1)

            def turned(b, g):
                act.wait_ge(s_wt, 4 * b + g + 1)
                tiles = 2 if g < 3 else 1
                fn(wT[b][:, 2 * g:2 * g + tiles, :].rearrange("p j n -> p (j n)"),
                   ABh[g % 2][:, 0:tiles * 2 * P], ACT.Copy).then_inc(s_wtev, 1)

            def chunk(b, j):
                if j in (1, 3):
                    turned(b, j // 2 + 2)

            def aT_(b, i):
                act.wait_ge(s_a, b + 1)
                fn(aT2[b][:, :], M0[:, :], ACT.Square).then_inc(s_aev, 1)
                fn(aT[b][:, :], M0[:, :], ACT.Copy).then_inc(s_aev, 1)
                half_root(b, 2)

            def q(b, i):
                if i == 0:
                    act.wait_ge(s_q, b + 1)
                    fn(sq[b][:, :, :].rearrange("p j d -> p (j d)"), M3[:, :], ACT.Square).then_inc(s_qsq, 1)
                else:
                    half_root(b, 3)

            def h2(b, i):
                act.wait_ge(s_h2, b + 1)
                fn(sq[b][:, :, :], h2c[b][:, :, :], ACT.Square).then_inc(s_h2sq, 1)

            def h3_(b, i):
                half_root(b, 4)
                act.wait_ge(s_h3t, b + 1)
                fn(h3T[b][:, :], ABh[0], ACT.Copy).then_inc(s_h3tev, 1)

            act.wait_ge(s_set, SET_WARM)
            fn(junk[:, :], warm[:, 0:1], ACT.Sqrt)
            mine = {"proj": proj, "retained": retained, "centre": centre, "norm": norm, "vt": vt, "dx": dx, "wt": turned,
                    "chunk": chunk, "aT": aT_, "q": q, "h2": h2, "h3": h3_}
            for stage, b, i in ORDER:
                if stage in mine:
                    mine[stage](b, i)
            for b in range(B):
                act.wait_ge(s_dl, b + 1)
                fn(ex[b][:, :, :], lg[b][:, :, :], ACT.Exp).then_inc(s_ex, 1)
            for p in range(PAIRS):
                act.wait_ge(s_xt, p + 1)
                fn(xbT[:, p, :, :, :].rearrange("d k g s -> d (k g s)"), AB[0:D, 0:2 * CAP], ACT.Copy).then_inc(s_xtev, 1)
                for g in range(2):
                    act.wait_ge(s_up, 4 * p + 2 * g + 1)
                    if p >= 2:
                        act.wait_ge(s_dn, p - 1)
                    a = PCOL["b1"][0] + 2 * (p + PAIRS * g)
                    fn(hm[:, p % 2, g, 0, :], UPB[2 * g][:, 0:CAP], ACT.Relu, bias=par[:, a:a + 1]).then_inc(s_hma, 1)

        @block.vector
        def _(dve):
            count = [0]

            def link(ins):
                count[0] += 1
                ins.then_inc(s_chain, 1)
                dve.wait_ge(s_chain, count[0])

            tt, tsc, stt = nc.vector.tensor_tensor, nc.vector.tensor_scalar, nc.vector.scalar_tensor_tensor
            reduce = nc.vector.tensor_reduce

            def inverse_root(b, k, dst):
                c = col_sb[b]
                v, half, r0, t = c[:, 25 + k, :], c[:, 30 + k, :], c[:, 35, :], c[:, 36, :]
                dve.wait_ge(s_root[k], b + 1)
                link(nc.vector.reciprocal(r0, half))
                link(tt(t, r0, v, ALU.mult))
                link(stt(t, t, 0.25, half, ALU.mult, ALU.add))
                link(nc.vector.reciprocal(dst, t))

            def score(b, i):
                s, f = divmod(i, 2)
                n = 2 * NT * b + i
                dve.wait_ge(d_gam[s], 16)
                dve.wait_ge(s_score, n + 1)
                if n >= NG:
                    dve.wait_ge(s_gv, (n - NG) // 2 + 1)
                tt(gs[:, n % NG, :], S[(21 * b + 5 + i) % 3][:, :], gam[:, s, hs(f)], ALU.mult).then_inc(s_gs, 1)

            def retained(b, i):
                if b > 0:
                    return
                dve.wait_ge(d_cst, 16)
                dve.wait_ge(d_par, 16)
                nc.vector.tensor_copy(tri_bf[:, :], ccol("tri")).then_inc(s_bfc, 1)
                nc.vector.memset(ones_bf[:, :], 1.0).then_inc(s_bfc, 1)
                et = pcol("et").rearrange("p (c d) -> p c d", c=2)
                link(reduce(et_mean[:, :], et, AX, ALU.add))
                link(tsc(et_mean[:, :], et_mean[:, :], 1.0 / D, None, ALU.mult))
                tt(etc[:, :, :], et, et_mean[:, :].unsqueeze(2).to_broadcast([P, 2, D]), ALU.subtract).then_inc(s_etc, 1)

            def prelu(b, i):
                dve.wait_ge(s_mix, b + 1)
                bo = pcol("bo").unsqueeze(1).to_broadcast([P, NT, D])
                tt(y1[b][:, :, :], M0[:, :].rearrange("p (j d) -> p j d", d=D), bo, ALU.add).then_inc(s_y, 1)
                dve.wait_ge(s_y, b + 1)
                link(tsc(y2[b][:, :, :], y1[b][:, :, :], 0.0, pcol("a"), ALU.min, ALU.mult))
                link(stt(h[b][:, :, :], y1[b][:, :, :], 0.0, y2[b][:, :, :], ALU.max, ALU.add))

            def centre(b, i):
                c = col_sb[b]
                link(reduce(c[:, 0, :], h[b][:, :, :], AX, ALU.add))
                link(tsc(c[:, 1, :], c[:, 0, :], 1.0 / D, None, ALU.mult))
                tt(hc[b][:, :, :], h[b][:, :, :], over(c[:, 1, :], D), ALU.subtract).then_inc(s_hc, 1)

            def norm(b, k):
                c = col_sb[b]
                if k == 0:
                    dve.wait_ge(s_hsq, b + 1)
                    link(reduce(c[:, 2, :], sq[b][:, :, :], AX, ALU.add))
                    tsc(c[:, 25, :], c[:, 2, :], 1.0 / D, LN_EPS, ALU.mult, ALU.add).then_inc(s_var[0], 1)
                    tsc(c[:, 3, :], c[:, 2, :], 1.0 / D, None, ALU.mult)
                    dve.wait_ge(s_var[0], b + 1)
                    inverse_root(b, 0, c[:, 4, :])
                    tt(vn[b][:, :, :], hc[b][:, :, :], over(c[:, 4, :], D), ALU.mult).then_inc(s_vn, 1)
                else:
                    link(tt(c[:, 5, :], c[:, 4, :], c[:, 4, :], ALU.mult))
                    link(tt(c[:, 5, :], c[:, 5, :], c[:, 3, :], ALU.mult))
                    tsc(c[:, 26, :], c[:, 5, :], LN_EPS, None, ALU.add).then_inc(s_var[1], 1)
                    dve.wait_ge(s_var[1], b + 1)

            def usum(b, i):
                c = col_sb[b]
                inverse_root(b, 1, c[:, 6, :])
                link(tt(c[:, 7, :], c[:, 4, :], c[:, 6, :], ALU.mult))
                dve.wait_ge(s_usum, b + 1)
                cm = c[:, 8, :].rearrange("p (f j) -> p j f", f=2)
                link(tsc(cm, M3[:, 0:NT].rearrange("p (j f) -> p j f", f=2), 1.0 / L1_EPS, 1.0, ALU.mult, ALU.min))
                nc.vector.tensor_tensor_scan(c[:, 9, :], ones8[:, :], c[:, 8, :], 0.0, ALU.mult, ALU.add).then_inc(s_cm, 1)

            def clamp(b, i):
                c = col_sb[b]
                U = M3[:, 0:NT]
                M = M3[:, NT:2 * NT].rearrange("p (f j) -> p j f", f=2)
                dve.wait_ge(s_m, b + 1)
                link(tsc(c[:, 10, :].rearrange("p (j f) -> p j f", f=2), M, 1.0, DECAY, ALU.min, ALU.mult))
                link(tt(c[:, 10, :], U, c[:, 10, :], ALU.add))
                link(tsc(c[:, 10, :], c[:, 10, :], L1_EPS, None, ALU.max))
                nc.vector.reciprocal(c[:, 11, :], c[:, 10, :]).then_inc(s_beta, 1)
                dve.wait_ge(s_beta, b + 1)
                link(stt(c[:, 20, :], c[:, 7, :], ccol("grow"), c[:, 11, :], ALU.mult, ALU.mult))
                tsc(c[:, 21, :], c[:, 20, :], TILE_DECAY, None, ALU.mult).then_inc(s_cl, 1)
                link(tsc(c[:, 12, :], c[:, 11, :], ccol("decay"), None, ALU.mult))

            def scan(b, i):
                dve.wait_ge(s_abc, b + 1)
                lo, hi = (1, HALF) if i == 0 else (HALF, T)
                for n in range(2):
                    nc.vector.tensor_tensor_scan(w[b][:, n, lo:hi], AB[:, lo - 1:hi - 1], w[b][:, n, lo:hi],
                                                 w[b][:, n, lo - 1:lo], ALU.mult, ALU.add).then_inc(s_w, 1)

            def at(b, i):
                mask = ccol("upper").unsqueeze(1).to_broadcast([P, 4, P])
                dve.wait_ge(s_at, 2 * b + i + 1)
                src = (M0 if i == 0 else M3)[:, :].rearrange("p (j t) -> p j t", t=P)
                tt(att[b][:, 4 * i:4 * i + 4, :], src, mask, ALU.mult).then_inc(s_att, 1)

            def chunk(b, j):
                if j == NT - 1:
                    return
                dve.wait_ge(s_c, (NT - 1) * b + j + 1)
                if j == 0:
                    nc.vector.tensor_copy(state[b][:, 1, :], M3[:, 0:2 * D]).then_inc(s_st, 1)
                else:
                    dve.wait_ge(s_st, (NT - 1) * b + j)
                    stt(state[b][:, j + 1, :], state[b][:, j, :], TILE_DECAY, M3[:, 0:2 * D],
                        ALU.mult, ALU.add).then_inc(s_st, 1)

            def aT_(b, i):
                c = col_sb[b]
                link(tt(c[:, 13, :], c[:, 12, :], c[:, 12, :], ALU.mult))
                dve.wait_ge(s_sa, b + 1)
                tt(c[:, 14, :], c[:, 13, :], M3[:, 0:NT], ALU.mult).then_inc(s_saev, 1)
                dve.wait_ge(s_saev, b + 1)
                tsc(c[:, 27, :], c[:, 14, :], 1.0 / D, LN_EPS, ALU.mult, ALU.add).then_inc(s_var[2], 1)

            def dy(b, n):
                dve.wait_ge(s_dy, 4 * b + n + 1)
                stt(yT[b][:, n // 2, hs(n % 2)], DYB[n], 0.0, w[b][:, n // 2, hs(n % 2)], ALU.max, ALU.mult).then_inc(s_yy, 1)

            def q(b, i):
                c = col_sb[b]
                if i == 0:
                    inverse_root(b, 2, c[:, 15, :])
                    link(tt(c[:, 16, :], c[:, 12, :], c[:, 15, :], ALU.mult))
                    link(tt(c[:, 16, :], c[:, 16, :], c[:, 11, :], ALU.mult))
                    link(tt(c[:, 17, :], c[:, 16, :], c[:, 16, :], ALU.mult))
                    dve.wait_ge(s_qsq, b + 1)
                    link(reduce(c[:, 18, :], sq[b][:, :, :], AX, ALU.add))
                    link(tt(c[:, 18, :], c[:, 18, :], c[:, 17, :], ALU.mult))
                    tsc(c[:, 28, :], c[:, 18, :], 1.0 / D, LN_EPS, ALU.mult, ALU.add).then_inc(s_var[3], 1)
                    dve.wait_ge(s_var[3], b + 1)
                else:
                    inverse_root(b, 3, c[:, 19, :])
                    link(tt(c[:, 19, :], c[:, 19, :], c[:, 16, :], ALU.mult))
                    tt(pq[b][:, :, :], M3[:, :].rearrange("p (j d) -> p j d", d=D), over(c[:, 19, :], D), ALU.mult).then_inc(s_p, 1)

            def h2(b, i):
                c = col_sb[b]
                dve.wait_ge(s_p, b + 1)
                tt(h2c[b][:, :, :], hc[b][:, :, :], pq[b][:, :, :], ALU.add).then_inc(s_h2, 1)
                dve.wait_ge(s_h2sq, b + 1)
                link(reduce(c[:, 22, :], sq[b][:, :, :], AX, ALU.add))
                tsc(c[:, 29, :], c[:, 22, :], 1.0 / D, LN_EPS, ALU.mult, ALU.add).then_inc(s_var[4], 1)
                dve.wait_ge(s_var[4], b + 1)

            def h3_(b, i):
                c = col_sb[b]
                inverse_root(b, 4, c[:, 23, :])
                tt(h3[b][:, :, :], h2c[b][:, :, :], over(c[:, 23, :], D), ALU.mult).then_inc(s_h3, 1)

            def gates(b, i):
                c = col_sb[b]
                dve.wait_ge(s_lg, b + 1)
                gb = pcol("gb").unsqueeze(1).to_broadcast([P, NT, NE])
                tt(lg[b][:, :, :], M3[:, 0:NT * NE].rearrange("p (j e) -> p j e", e=NE), gb, ALU.add).then_inc(s_lgev, 1)
                dve.wait_ge(s_lgev, b + 1)
                link(reduce(c[:, 24, :], lg[b][:, :, :], AX, ALU.max))
                tt(lg[b][:, :, :], lg[b][:, :, :], over(c[:, 24, :], NE), ALU.subtract).then_inc(s_dl, 1)
                dve.wait_ge(s_dl, b + 1)
                first = ccol("first").rearrange("p (j e) -> p j e", e=NE)
                link(stt(key[b][:, :, :], lg[b][:, :, :], 0.0, first, ALU.is_equal, ALU.mult))
                link(reduce(c[:, 37, :], key[b][:, :, :], AX, ALU.max))
                tt(oh[b][:, :, :], key[b][:, :, :], over(c[:, 37, :], NE), ALU.is_equal).then_inc(s_oh, 1)
                dve.wait_ge(s_oh, b + 1)
                base = ccol("base").rearrange("p (j e) -> p j e", e=NE)
                link(tt(key[b][:, :, :], oh[b][:, :, :], base, ALU.mult))
                link(reduce(c[:, 38, :], key[b][:, :, :], AX, ALU.add))

            def slots(b, i):
                c = col_sb[b]
                dve.wait_ge(s_cum, b + 1)
                v4 = "p (j f) e -> p j f e"
                tt(key[b][:, :, :].rearrange(v4, f=2), M0[:, 0:NT * NE].rearrange("p (f j e) -> p j f e", f=2, e=NE),
                   oh[b][:, :, :].rearrange(v4, f=2), ALU.mult).then_inc(s_cumev, 1)
                dve.wait_ge(s_cumev, b + 1)
                link(reduce(c[:, 39, :], key[b][:, :, :], AX, ALU.add))
                link(stt(c[:, 38, :], c[:, 39, :], -1.0, c[:, 38, :], ALU.add, ALU.add))
                link(tsc(c[:, 39, :], c[:, 39, :], float(CAP), float(2 * SLOTS), ALU.is_gt, ALU.mult))
                tt(slot_i[b][:, :], c[:, 38, :], c[:, 39, :], ALU.add).then_inc(s_slot, 1)

            def probabilities(b):
                c = col_sb[b]
                dve.wait_ge(s_ex, b + 1)
                link(reduce(c[:, 0, :], ex[b][:, :, :], AX, ALU.add))
                link(nc.vector.reciprocal(c[:, 2, :], c[:, 0, :]))
                link(tt(fin[b][:, :, :], h2c[b][:, :, :], over(c[:, 1, :], D), ALU.add))

            def hidden(p):
                for g in range(2):
                    dve.wait_ge(s_up, 4 * p + 2 * g + 2)
                    if p >= 2:
                        dve.wait_ge(s_dn, p - 1)
                    a = PCOL["b1"][0] + 2 * (p + PAIRS * g) + 1
                    tsc(hm[:, p % 2, g, 1, :], UPB[2 * g + 1][:, 0:CAP], par[:, a:a + 1], 0.0, ALU.add, ALU.max).then_inc(s_hmd, 1)

            def result(p):
                dve.wait_ge(s_dn, p + 1)
                a = PCOL["b2"][0] + p * D
                b2 = par[:, a:a + D].unsqueeze(1).to_broadcast([P, KS, D])
                src = (R if p % 2 == 0 else M3)[:, 0:CAP].rearrange("p (k d) -> p k d", d=D)
                tt(yb_sb[:, p, :, :], src, b2, ALU.add).then_inc(s_yb, 1)

            def finish(n, b, first, tiles):
                c = col_sb[b]
                t4 = slice(first, first + tiles)
                y, pos, mask, rep = yg[b][:, t4, :], fpos[:, 0:tiles, :], fmask[:, 0:tiles, :], frep[:, 0:tiles, :]
                z = fin[b][:, t4, :]
                dve.wait_ge(d_gather[n], 16 * tiles)
                link(tt(y, y, c[:, 2, t4].unsqueeze(2).to_broadcast([P, tiles, D]), ALU.mult))
                link(tsc(pos, y, 0.0, None, ALU.max))
                link(stt(y, y, 0.0, pos, ALU.min, ALU.add))
                tsc(rep, y, 1e4, -1e4, ALU.min, ALU.max)
                link(tsc(mask, y, 0.0, 0.0, ALU.mult, ALU.is_equal))
                link(nc.vector.copy_predicated(rep, mask, y))
                tt(z, z, rep, ALU.add).then_inc(s_fin, 1)

            link(nc.vector.memset(ones8[:, :], 1.0))
            mine = {"score": score, "retained": retained, "prelu": prelu, "centre": centre, "norm": norm, "usum": usum,
                    "clamp": clamp, "scan": scan, "at": at, "chunk": chunk, "aT": aT_, "dy": dy, "q": q, "h2": h2, "h3": h3_,
                    "gate": gates, "slots": slots}
            for stage, b, i in ORDER:
                if stage in mine:
                    mine[stage](b, i)
            for b in range(B):
                probabilities(b)
            for p in range(PAIRS):
                hidden(p)
                if p > 0:
                    result(p - 1)
            result(PAIRS - 1)
            for n, (b, first, tiles) in enumerate(GROUPS):
                finish(n, b, first, tiles)

        @block.tensor
        def _(pe):
            mm = nc.tensor.matmul

            def bank_free(n):
                mb, i = divmod(n - 3, 21)
                if mb < 0:
                    return
                if i < 5:
                    pe.wait_ge(s_projev, 5 * mb + i + 1)
                else:
                    pe.wait_ge(s_gs, 16 * mb + i - 5 + 1)

            def proj(b, i):
                if i == 0:
                    pe.wait_ge(d_wa, 16)
                    pe.wait_ge(d_x[b], 16)
                n = 21 * b + i
                bank_free(n)
                if i < 4:
                    mm(S[n % 3][:, :], wa_sb[:, (i % 2) * P:(i % 2 + 1) * P], x_sb[b][:, hs(i // 2)],
                       start=True, stop=True).then_inc(s_proj, 1)
                else:
                    for j in range(NT):
                        last = mm(S[n % 3][:, j * D:(j + 1) * D], x_sb[b][:, ts(j)], wa_sb[:, 4 * D:5 * D], start=True, stop=True)
                    last.then_inc(s_proj, 1)

            def retained_part(b, s):
                if s == 0 and b > 0:
                    pe.wait_ge(s_ret, b)
                pe.wait_ge(s_gs, 16 * b + 2 * s + 2)
                for f in range(2):
                    last = mm(R[D * f:D * f + D, :], v_sb[b][:, s, :], gs[:, (16 * b + 2 * s + f) % NG, :],
                              start=(s == 0), stop=(s == NT - 1))
                last.then_inc(s_gv, 1)

            def score(b, i):
                s, f = divmod(i, 2)
                if i == 0:
                    pe.wait_ge(s_projev, 5 * b + 5)
                n = 21 * b + 5 + i
                bank_free(n)
                mm(S[n % 3][:, :], k_sb[b][D * f:D * f + D, ts(s)], q_sb[b][D * f:D * f + D, hs(f)],
                   start=True, stop=True).then_inc(s_score, 1)
                if f == 1 and s >= 1:
                    retained_part(b, s - 1)

            def retained(b, i):
                retained_part(b, NT - 1)

            def wo(b, i):
                pe.wait_ge(s_ret, b + 1)
                if b == 0:
                    pe.wait_ge(d_par, 16)
                    pe.wait_ge(d_cst, 16)
                    pe.wait_ge(s_set, SET_BIG)
                else:
                    pe.wait_ge(s_cumev, b)
                for j in range(4):
                    last = mm(M0[:, ts(j)], ret[b][:, ts(j)], pcol("wo"), start=True, stop=True)
                last.then_inc(s_mix, 1)

            def vt(b, i):
                pe.wait_ge(s_vn, b + 1)
                if b > 0:
                    pe.wait_ge(s_h3tev, b)
                for j in range(4):
                    last = nc.tensor.transpose(ABh[0][:, ts(j)], vn[b][:, 2 * j:2 * j + 2, :].rearrange("p f d -> p (f d)"), ccol("ident"))
                last.then_inc(s_vt, 1)

            def dx(b, n):
                if n == 0:
                    pe.wait_ge(s_vtev, b + 1)
                if n == 0:
                    pe.wait_ge(s_y, b + 1)
                if n == 1 and b > 0:
                    pe.wait_ge(s_lgev, b)
                a = PCOL["dxt"][0] + n // 2 * P
                f = n % 2
                mm(DXB[n], par[D * f:D * f + D, a:a + P], vT[b][D * f:D * f + D, :], start=True, stop=True).then_inc(s_dx, 1)

            def usum(b, i):
                pe.wait_ge(s_u, 4 * b + 4)
                for tau in range(NT):
                    for c in range(2):
                        last = mm(M3[:, place(tau):place(tau) + 1], w[b][:, c, ts(tau)], ones[:, :], start=(c == 0), stop=(c == 1))
                last.then_inc(s_usum, 1)

            def clamp(b, i):
                pe.wait_ge(s_cm, b + 1)
                cm, run = col_sb[b][:, 8, :], col_sb[b][:, 9, :]
                mm(M3[:, NT:2 * NT], ccol("near"), cm, start=True, stop=False)
                mm(M3[:, NT + 1:2 * NT], ccol("prev"), cm[:, 0:NT - 1], start=False, stop=False)
                mm(M3[:, NT + 2:2 * NT], big[:, :], run[:, 0:NT - 2], start=False, stop=True).then_inc(s_m, 1)

            def beta(b, i):
                pe.wait_ge(s_beta, b + 1)
                for tau in range(NT):
                    k = place(tau)
                    last = mm(ABh[tau // 4][:, ts(tau % 4)], col_sb[b][:, 11, k:k + 1].to_broadcast([P, P]), ccol("ident97"),
                              start=True, stop=True)
                last.then_inc(s_abc, 1)

            def at(b, i):
                pe.wait_ge(s_w, 4 * b + 2 * i + 2)
                if i == 0:
                    pe.wait_ge(s_u, 4 * b + 1)
                if i == 1:
                    pe.wait_ge(s_beta, b + 1)
                for tau in range(4 * i, 4 * i + 4):
                    for c in range(2):
                        last = mm((M0 if i == 0 else M3)[:, ts(tau % 4)], w[b][:, c, ts(tau)], w[b][:, c, ts(tau)],
                                  start=(c == 0), stop=(c == 1))
                last.then_inc(s_at, 1)

            def turned(b, g):
                if g >= 2:
                    pe.wait_ge(s_wtev, 4 * b + g - 1)
                else:
                    pe.wait_ge(s_w, 4 * b + 4)
                for j in range(2 * g, min(2 * g + 2, NT - 1)):
                    for c in range(2):
                        at_ = (j % 2) * 2 * P + c * P
                        last = nc.tensor.transpose(ABh[g % 2][:, at_:at_ + P], w[b][:, c, ts(j)], ccol("ident"))
                last.then_inc(s_wt, 1)

            def chunk(b, j):
                if j == 0:
                    pe.wait_ge(s_att, 2 * b + 2)
                if j in (1, 3):
                    turned(b, j // 2 + 2)
                if j < NT - 1:
                    pe.wait_ge(s_lb, 2 * b + 1)
                    pe.wait_ge(s_wtev, 4 * b + j // 2 + 1)
                    if j > 0:
                        pe.wait_ge(s_st, (NT - 1) * b + j)
                    for c in range(2):
                        last = mm(M3[:, c * D:(c + 1) * D], wT[b][:, j, ts(c)], lbc[b][:, place(j), :], start=True, stop=True)
                    last.then_inc(s_c, 1)
                f = j // 4
                dst = M0[D * f:D * f + D, ts(j % 4)]
                pe.wait_ge(s_lb, 2 * b + 2)
                last = mm(dst, lb[b][:, place(j), :], att[b][:, j, :], start=True, stop=(j == 0))
                if j > 0:
                    pe.wait_ge(s_st, (NT - 1) * b + j)
                    for c in range(2):
                        last = mm(dst, state[b][:, j, c * D:(c + 1) * D], w[b][:, c, ts(j)], start=False, stop=(c == 1))
                if j == NT - 1:
                    last.then_inc(s_a, 1)

            def aT_(b, i):
                pe.wait_ge(s_aev, 2 * b + 1)
                pe.wait_ge(s_st, (NT - 1) * (b + 1))
                for j in range(4):
                    last = mm(M3[:, 2 * j:2 * j + 2], aT2[b][:, ts(j)], ccol("halves"), start=True, stop=True)
                last.then_inc(s_sa, 1)

            def dy(b, n):
                if n == 0:
                    pe.wait_ge(s_aev, 2 * b + 2)
                    pe.wait_ge(s_wtev, 4 * b + 4)
                if n == 3:
                    pe.wait_ge(s_yy, 4 * b + 1)
                a = PCOL["dyt"][0] + n // 2 * P
                f = n % 2
                mm(DYB[n], par[D * f:D * f + D, a:a + P], aT[b][D * f:D * f + D, :], start=True, stop=True).then_inc(s_dy, 1)

            def q(b, i):
                if i == 1:
                    return
                pe.wait_ge(s_etc, 1)
                pe.wait_ge(s_saev, b + 1)
                pe.wait_ge(s_yy, 4 * b + 4)
                for tau in range(NT):
                    for c in range(2):
                        k = place(tau)
                        last = mm(M3[:, k * D:(k + 1) * D], yT[b][:, c, ts(tau)], etc[:, c, :], start=(c == 0), stop=(c == 1))
                last.then_inc(s_q, 1)

            def h3_(b, i):
                pe.wait_ge(s_h3, b + 1)
                for j in range(4):
                    last = nc.tensor.transpose(ABh[0][:, ts(j)], h3[b][:, 2 * j:2 * j + 2, :].rearrange("p f d -> p (f d)"), ccol("ident"))
                last.then_inc(s_h3t, 1)

            def gates(b, i):
                pe.wait_ge(s_h3tev, b + 1)
                pe.wait_ge(s_p, b + 1)
                pe.wait_ge(s_qsq, b + 1)
                for j in range(4):
                    last = mm(M3[:, 2 * j * NE:(2 * j + 2) * NE], h3T[b][:, ts(j)], pcol("gate"), start=True, stop=True)
                last.then_inc(s_lg, 1)

            def slots(b, i):
                pe.wait_ge(s_bfc, 2)
                pe.wait_ge(s_oh, b + 1)
                terms = [(M0[:, 0:NT * NE].rearrange("p (f j e) -> p f j e", f=2, e=NE), tri_bf,
                          oh[b][:, :, :].rearrange("p (j f) e -> p f j e", f=2))]
                for tau in range(NT - 1):
                    k, n = place(tau), NT - 1 - tau
                    terms.append((M0[:, (tau + 1) * NE:NT * NE].rearrange("p (j e) -> p j e", e=NE), ones_bf,
                                  oh[b][:, k:k + 1, :].to_broadcast([P, n, NE])))
                for a in range(b):
                    for k in range(NT):
                        terms.append((M0[:, 0:NT * NE].rearrange("p (j e) -> p j e", e=NE), ones_bf,
                                      oh[a][:, k:k + 1, :].to_broadcast([P, NT, NE])))
                for n, (dst, lhs, rhs) in enumerate(terms):
                    last = mm(dst, lhs[:, :], rhs, start=(n == 0), stop=(n == len(terms) - 1))
                last.then_inc(s_cum, 1)

            pe.wait_ge(s_set, SET_WARM)
            for i in range(WARM):
                mm(M0[:, :], warm[:, 0:P], warm[:, :], start=True, stop=True)
            mine = {"proj": proj, "score": score, "retained": retained, "wo": wo, "vt": vt, "dx": dx, "usum": usum, "clamp": clamp,
                    "beta": beta, "at": at, "wt": turned, "chunk": chunk, "aT": aT_, "dy": dy, "q": q, "h3": h3_,
                    "gate": gates, "slots": slots}
            for stage, b, i in ORDER:
                if stage in mine:
                    mine[stage](b, i)

            def slots_turned(p):
                pe.wait_ge(d_xb[p], 32)
                if p >= 1:
                    pe.wait_ge(s_xtev, p)
                for k in range(KS):
                    last = nc.tensor.transpose(AB[0:D, k * P:(k + 1) * P], xb[:, p, k, :], ccol("ident"))
                last.then_inc(s_xt, 1)

            def up(p):
                pe.wait_ge(s_xtev, p + 1)
                for g in range(2):
                    for c in range(2):
                        if p > 0:
                            pe.wait_ge(s_hma if c == 0 else s_hmd, 2 * (p - 1) + g + 1)
                        mm(UPB[2 * g + c][:, 0:CAP], w1_sb[:, p + PAIRS * g, ts(c)], xbT[:, p, :, g, :],
                           start=True, stop=True).then_inc(s_up, 1)

            def down(p):
                pe.wait_ge(s_hma, 2 * p + 2)
                pe.wait_ge(s_hmd, 2 * p + 2)
                if p >= 2:
                    pe.wait_ge(s_yb, p - 1)
                bank = R if p % 2 == 0 else M3
                for k in range(KS):
                    for c in range(2):
                        for g in range(2):
                            last = mm(bank[64 * g:64 * g + 64, k * D:(k + 1) * D], hm[:, p % 2, g, c, k * D:(k + 1) * D],
                                      w2_sb[:, p + PAIRS * g, c, :], start=(c == 0), stop=(c == 1))
                last.then_inc(s_dn, 1)

            pe.wait_ge(s_h3tev, B)
            pe.wait_ge(s_cumev, B)
            pe.wait_ge(s_lgev, B)
            pe.wait_ge(s_gs, 16 * B)
            pe.wait_ge(s_ret, B)
            pe.wait_ge(d_w1, 16)
            pe.wait_ge(d_w2, 16)
            slots_turned(0)
            for p in range(PAIRS):
                up(p)
                if p + 1 < PAIRS:
                    slots_turned(p + 1)
                if p > 0:
                    down(p - 1)
            down(PAIRS - 1)


def constants(np):
    out = np.zeros((P, CWIDTH), np.float32)

    def put(name, value):
        out[:, CCOL[name][0]:CCOL[name][1]] = value
    s, t = np.arange(P)[:, None], np.arange(P)[None, :]
    put("ident", (s == t))
    put("ident97", DECAY * (s == t))
    put("upper", (s < t))
    put("tri", (s <= t))

    def power(k):
        return np.where(k >= 3, BIG, (DECAY / L1_EPS) ** np.clip(k, 0, 2).astype(np.float64))
    put("near", np.where(s < t, power(t - 1 - s), 0.0))
    put("prev", power(t - 1 - s + P))
    put("grow", DECAY ** -(s + 1.0))
    put("decay", DECAY ** (s * 1.0))
    e = np.arange(NT * NE)[None, :] % NE
    put("first", (NE - e) * np.ones((P, 1)))
    put("base", (CAP * e) * np.ones((P, 1)))
    put("halves", np.arange(2)[None, :] == s // D)
    return out


def kernel(**inputs):
    import numpy as np
    import concourse.bacc as bacc
    from concourse.bass_utils import run_bass_kernel_spmd

    g = {k: np.asarray(v) for k, v in inputs.items()}
    f = np.float32
    x = g["x"].reshape(B, T, D)
    xT = np.concatenate([x.transpose(0, 2, 1), np.ones((B, 1, T), f)], axis=1)
    rows = lambda w, b: np.concatenate([g[w], g[b][None, :]], axis=0)
    q, k, v = rows("L0_tok_Wq", "L0_tok_bq"), rows("L0_tok_Wk", "L0_tok_bk"), rows("L0_tok_Wv", "L0_tok_bv")
    wa = np.concatenate([q, q, k, k, v], axis=1)
    gammaT = g["L0_tok_d_gamma_batched"].T.reshape(NT, P, T)
    params = np.zeros((P, PWIDTH), f)

    def put(name, value, hi=P):
        params[0:hi, PCOL[name][0]:PCOL[name][1]] = value
    def on_both_halves(w):
        out = np.zeros((2 * w.shape[0], 2 * w.shape[1]), f)
        out[:w.shape[0], :w.shape[1]] = w
        out[w.shape[0]:, w.shape[1]:] = w
        return out
    put("wo", on_both_halves(g["L0_tok_Wo"]))
    put("gate", on_both_halves(g["L0_ffn_gate_w"]))
    put("gb", g["L0_ffn_gate_b"][None, :])
    put("bo", g["L0_tok_bo"][None, :])
    put("dxt", np.concatenate([g["L0_attn_Dx"].T] * 2, axis=0))
    put("dyt", np.concatenate([g["L0_attn_Dy"].T] * 2, axis=0))
    put("et", g["L0_attn_E"].T.reshape(2, P, D).transpose(1, 0, 2).reshape(P, 2 * D))
    put("a", g["L0_tok_prelu_a"].reshape(1, 1))
    put("b1", g["L0_ffn_b1"].reshape(NE * 2, P).T)
    b2 = g["L0_ffn_b2"].reshape(2, 1, PAIRS * D)
    put("b2", np.broadcast_to(b2, (2, 64, PAIRS * D)).reshape(P, PAIRS * D))
    arrays = {"xT": xT, "wa": wa, "gammaT": gammaT, "params": params, "consts": constants(np), 
              "w1": g["L0_ffn_w1"], "w2": g["L0_ffn_w2"]}
    arrays = {n: np.ascontiguousarray(a, dtype=f) for n, a in arrays.items()}

    nc = bacc.Bacc("TRN2", target_bir_lowering=False, num_devices=1)
    f32 = mybir.dt.float32
    aps = {n: nc.dram_tensor(n, a.shape, f32, kind="ExternalInput").ap() for n, a in arrays.items()}
    out = nc.dram_tensor("out", (B, T, D), f32, kind="ExternalOutput").ap()
    slots_in = nc.dram_tensor("slots_in", (SLOTS, D), f32, kind="Internal").ap()
    slots_out = nc.dram_tensor("slots_out", (SLOTS, D), f32, kind="Internal").ap()
    build(nc, out=out, slots_in=slots_in, slots_out=slots_out, **aps)
    r = run_bass_kernel_spmd(nc, [arrays], core_ids=[0])
    return r.results[0]["out"]
```

```python
import concourse.bass as bass
from concourse import mybir
from contextlib import ExitStack

B, T, D = 2, 1024, 64
N = 256
NE, F = 8, 256
P = 128
NT = T // P
HALF = T // 2
CAP = (5 * B * T) // (4 * NE)
SLOTS = NE * CAP
KS = CAP // 64
PAIRS = NE // 2
DECAY = 0.97
TILE_DECAY = DECAY ** P
WARM = 6
WARM_BLOCKS, WARM_BLOCK = 5, 8
LN_EPS, L1_EPS = 1e-5, 1e-12
BIG = 1e35

PROJ = [("wq", 2 * D), ("wk", 2 * D), ("wv", D), ("bq", 1), ("bk", 1), ("bv", D)]
PARAMS = [("wo", 2 * D), ("bo", 2 * D), ("dxt", N), ("dyt", N), ("et", 2 * D), ("a", 1), ("b1", 2 * NE), ("b2", PAIRS * D), ("gate", 2 * NE), ("gb", NE)]
CONSTS = [("ident", P), ("ident97", P), ("upper", P), ("tri", P), ("near", P), ("prev", P),
          ("grow", 1), ("decay", 1), ("first", NT * NE), ("base", NT * NE), ("halves", 2)]


def place(tau):
    return 2 * (tau % 4) + tau // 4


GROUPS = [(0, 0, 8), (1, 0, 4), (1, 4, 2), (1, 6, 2)]


RECURRENCE = ([("wo", 0), ("prelu", 0), ("centre", 0), ("norm", 0), ("inverse", 0), ("norm", 1), ("vt", 0), ("vt", 1)]
              + [("dx", n) for n in range(4)]
              + [("usum", 0), ("usum", 1), ("clamp", 0), ("beta", 0), ("scan", 0), ("at", 0), ("scan", 1),
                 ("at", 1), ("wt", 0), ("wt", 1), ("grow", 0), ("wt", 2), ("wt", 3)]
              + [("chunk", j) for j in range(4)] + [("grow", 1)] + [("chunk", j) for j in range(4, NT)] + [("aT", 0)] + [("dy", n) for n in range(4)] + [("scale", 0)]
              + [("q", 0), ("q", 1), ("h2", 0), ("variance", 0), ("h3", 0), ("gate", 0), ("slots", 0)])
EXPERTS = [sum([[("xt", p), ("up", p), ("down", p)] for p in range(PAIRS)], []) + [("gather", 0)],
           [("warm", i) for i in range(WARM_BLOCKS)] + [("xt", 0)]
           + sum([[("xt", p + 1)] * (p + 1 < PAIRS) + [("up", p)] + [("down", p - 1)] * (p > 0) for p in range(PAIRS)], [])
           + [("down", PAIRS - 1), ("gather", 0)]]
TURNS = [(15, 2), (8, 2), (6, 1), (1, 1), (1, 6), (1, 2), (1, 2), (2, 4), (2, 3), (1, 1), (1, 1), (2, 2), (2, 3), (1, 2),
         (2, 1), (1, 1), (2, 1), (1, 1), (1, 2), (2, 1), (2, 2), (3, 2), (4, 1), (2, 1), (1, 2), (1, 1), (1, 1), (2, 6),
         (1, 7), (1, 6), (1, 1), (1, 1), (3, 1), (3, 1), (2, 1), (2, 4), (1, 12), (1, 4)]


def mixing_units(b):
    return ([("proj", b, i) for i in range(4)] + [("score", b, 0), ("score", b, 1), ("proj", b, 4)]
            + [("score", b, i) for i in range(2, 2 * NT)])


UNITS = {(b, name, i): n + b * (2 * NT + 5) for b in range(B) for n, (name, _, i) in enumerate(mixing_units(b))}
UNIT_LIST = sum([mixing_units(b) for b in range(B)], [])


def batch_stages(b):
    out = [("x", 0), ("x", 1)] + [(name, i) for name, _, i in mixing_units(b)] + [("retained", 0)] + RECURRENCE
    out += [("prob", 0)] * b + EXPERTS[b] + [("finish", n) for n, group in enumerate(GROUPS) if group[0] == b]
    return [(name, b, i) for name, i in out]


def program_order():
    out, left = [], [batch_stages(b) for b in range(B)]
    for turn in TURNS:
        for b in range(B):
            out, left[b] = out + left[b][:turn[b]], left[b][turn[b]:]
    return out


ORDER = program_order()


def columns(table):
    at, out = 0, {}
    for name, width in table:
        out[name] = (at, at + width)
        at += width
    return out, at


ACOL, AWIDTH = columns(PROJ)
PCOL, PWIDTH = columns(PARAMS)
CCOL, CWIDTH = columns(CONSTS)


def build(nc, x2, wa, gammaT, params, consts, w1, w2, out, slots_in, slots_out):
    f32, f32r, bf16, i32 = mybir.dt.float32, mybir.dt.float32r, mybir.dt.bfloat16, mybir.dt.int32
    ALU = mybir.AluOpType
    ACT = mybir.ActivationFunctionType
    AX = mybir.AxisListType.X

    ctx = ExitStack()
    with ctx:
        def sb(name, shape, dt=f32):
            return ctx.enter_context(nc.sbuf_tensor(name, shape, dt))

        def pb(name, shape, dt=f32):
            return ctx.enter_context(nc.psum_tensor(name, shape, dt))

        def sem(name):
            return ctx.enter_context(nc.semaphore(name))

        def ts(j):
            return slice(j * P, (j + 1) * P)

        def hs(i):
            return slice(i * HALF, (i + 1) * HALF)

        def both(name, shape, dt=f32):
            return [sb(f"{name}_{b}", shape, dt) for b in range(B)]

        def small(name):
            return [sb(name, [P, NT, D]), small_room(name).rearrange("p (j d) -> p j d", d=D)]

        def flat(name):
            return [sb(name, [P, HALF]), small_room(name)]

        def small_room(name):
            k = small_used[0]
            small_used[0] += 1
            if k < NG:
                return gs[:, k, :]
            if k < NG + 4:
                return x_sb[(k - NG) // 2][:, hs(k % 2)]
            return sb(name + "_1", [P, HALF])[:, :]

        def in_gamma(name, shape, lo, pattern, **sizes):
            chunks = shape[1] * shape[2] // T
            view = gam[:, lo:lo + chunks, :] if pattern is None else gam[:, lo:lo + chunks, :].rearrange("p a t -> p (a t)").rearrange(pattern, **sizes)
            return [sb(name, shape), view]

        x_sb = both("x_sb", [P, T])
        x_hi = sb("x_hi", [P, T], f32r)
        x_lo = sb("x_lo", [P, T], f32r)
        wa_sb = sb("wa_sb", [P, AWIDTH])
        wa_hilo = sb("wa_hilo", [P, 5 * D], f32r)
        dx_hilo = sb("dx_hilo", [P, N], f32r)
        gam = sb("gam", [P, NT, T])
        par = sb("par", [P, PWIDTH])
        cst = sb("cst", [P, CWIDTH])
        warm = sb("warm", [P, HALF], bf16)
        w1_hilo = sb("w1_hilo", [P, NE, F], f32r)
        w2_sb = sb("w2_sb", [P, NE, 2, D])
        ones = sb("ones", [P, 1])
        ones_row = sb("ones_row", [1, P])
        ones8 = sb("ones8", [P, NT])
        junk = sb("junk", [P, 1])
        big = sb("big", [P, P])
        tri_bf = sb("tri_bf", [P, P], bf16)
        ones_bf = sb("ones_bf", [P, P], bf16)
        etc = sb("etc", [P, 2, D])
        et_mean = sb("et_mean", [P, 2])

        xbT_hi = sb("xbT_hi", [P, 2, KS, 2, D], f32r)
        xbT_lo = sb("xbT_lo", [P, 2, KS, 2, D], f32r)
        hm_all = sb("hm_all", [P, 8 * CAP])
        hm = hm_all[:, :].rearrange("p (a g c t) -> p a g c t", a=2, g=2, c=2)
        w1_raw = hm_all[:, 0:NE * F].rearrange("p (e f) -> p e f", e=NE)

        q_hi = sb("q_hi", [P, T], f32r)
        q_lo = sb("q_lo", [P, T], f32r)
        k_hilo = sb("k_hilo", [P, T], f32r)
        v_sb = sb("v_sb", [P, NT, D])
        NG = 6
        gs = sb("gs", [P, NG, HALF])
        small_used = [0]
        vh = [sb("vh", [P, T], f32r), q_hi]
        vl = [sb("vl", [P, T], f32r), q_lo]
        ret, aT, aT2, h3T = flat("ret"), flat("aT"), flat("aT2"), flat("h3T")
        fin, h, hc, sq, lb, lbc, pq = (small(n) for n in ("fin", "h", "hc", "sq", "lb", "lbc", "pq"))
        w = in_gamma("w_all", [P, 2, T], 0, None)
        yT = in_gamma("yT", [P, 2, T], 2, None)
        wT = in_gamma("wT", [P, NT, 2 * P], 4, "p (j n) -> p j n", n=2 * P)
        att = in_gamma("att", [P, NT, P], 6, "p (j t) -> p j t", t=P)
        state = in_gamma("state", [P, NT, 2 * D], 7, "p (j t) -> p j t", t=2 * D)
        vn = [att[b][:, :, :].rearrange("p j (g d) -> p j g d", g=2) for b in range(B)]
        flat_ = "p a t -> p (a t)"
        xb = [(w[0][:, :, :] if p == 3 else wT[0][:, :, :]).rearrange(flat_)[:, p % 3 * KS * P:(p % 3 + 1) * KS * P]
              .rearrange("p (k g d) -> p k g d", k=KS, g=2) for p in range(PAIRS)]
        yb_sb = yT[0][:, :, :].rearrange(flat_)[:, 0:PAIRS * KS * D].rearrange("p (a k d) -> p a k d", a=PAIRS, k=KS)
        fpos, frep, fmask = sq[0], lbc[0], lb[0][:, :, :].bitcast(i32)
        h2c = both("h2c", [P, NT, D])
        h3 = both("h3", [P, NT, D])
        lg = both("lg", [P, NT, NE])
        ex = both("ex", [P, NT, NE])
        key = both("key", [P, NT, NE])
        oh = both("oh", [P, NT, NE], bf16)
        slot_i = both("slot_i", [P, NT], i32)
        yg = both("yg", [P, NT, D])
        NC = 40
        col_sb = both("col_sb", [P, NC, NT])

        ring2 = pb("S01", [P, T])
        S2 = pb("S2", [P, HALF])
        S = [ring2[:, 0:HALF], ring2[:, HALF:T], S2[:, :]]
        R = pb("R", [P, HALF])
        M0 = [pb("M0", [P, HALF]), S2]
        M3 = [pb("M3", [P, HALF]), R]
        AB = [pb("AB", [P, T]), ring2]
        ABh = [[AB[b][:, 0:HALF], AB[b][:, HALF:T]] for b in range(B)]

        def pcol(name, lo=0, hi=P):
            a, z = PCOL[name]
            return par[lo:hi, a:z]

        def ccol(name):
            a, z = CCOL[name]
            return cst[:, a:z]

        DXB = [[M0[b][:, :], M3[b][:, :], ABh[b][0], ABh[b][1]] for b in range(B)]
        DYB = [[ABh[b][0], ABh[b][1], M0[b][:, :], ABh[b][0]] for b in range(B)]
        XTB = AB[0][:, 0:KS * P]
        UPB = [[M0[0][:, :], ABh[0][0], ABh[0][1], M0[0][:, :]], [S2[:, :], ring2[:, 0:HALF], ring2[:, HALF:T], M0[0][:, :]]]
        DNB = [[M3[0][:, 0:CAP]], [R[:, 0:CAP], M3[0][:, 0:CAP]]]

        def over(col, n):
            return col.unsqueeze(2).to_broadcast([P, NT, n])

        d_x = [sem(f"d_x{b}") for b in range(B)]
        d_wa, d_par, d_cst, d_w1, d_w2 = (sem(n) for n in ("d_wa", "d_par", "d_cst", "d_w1", "d_w2"))
        d_gam = [sem(f"d_gam{i}") for i in range(NT)]
        d_zero, d_out = sem("d_zero"), sem("d_out")
        d_scatter = [sem(f"d_scatter{b}") for b in range(B)]
        d_xb = [[sem(f"d_xb{b}{p}") for p in range(PAIRS)] for b in range(B)]
        d_yb = [sem(f"d_yb{b}") for b in range(B)]
        d_gather = [sem(f"d_gather{g}") for g in range(len(GROUPS))]
        s_set = sem("s_set")
        s_bfc = sem("s_bfc")
        s_etc = sem("s_etc")
        s_whi, s_wlo = sem("s_whi"), sem("s_wlo")
        s_w1lo = sem("s_w1lo")
        s_xhi, s_xlo = sem("s_xhi"), sem("s_xlo")
        s_proj, s_hi, s_lo, s_v = sem("s_proj"), sem("s_hi"), sem("s_lo"), sem("s_v")
        s_score, s_gs, s_gv = sem("s_score"), sem("s_gs"), sem("s_gv")
        s_ret, s_mix, s_y = sem("s_ret"), sem("s_mix"), sem("s_y")
        s_hc, s_hsq = sem("s_hc"), sem("s_hsq")
        s_var = [sem(f"s_var{k}") for k in range(5)]
        s_root = [sem(f"s_root{k}") for k in range(5)]
        s_r = sem("s_r")
        s_vn2 = sem("s_vn2")
        s_vn, s_vt, s_vhi, s_vlo = sem("s_vn"), sem("s_vt"), sem("s_vhi"), sem("s_vlo")
        s_dx, s_u, s_us = sem("s_dx"), sem("s_u"), sem("s_us")
        s_usum, s_cm, s_m, s_beta = sem("s_usum"), sem("s_cm"), sem("s_m"), sem("s_beta")
        s_abc, s_w = sem("s_abc"), sem("s_w")
        s_cl, s_lb = sem("s_cl"), sem("s_lb")
        s_at, s_att = sem("s_at"), sem("s_att")
        s_wt, s_wtev = sem("s_wt"), sem("s_wtev")
        s_c, s_st = sem("s_c"), sem("s_st")
        s_a, s_aev = sem("s_a"), sem("s_aev")
        s_sa, s_saev = sem("s_sa"), sem("s_saev")
        s_dy, s_yy = sem("s_dy"), sem("s_yy")
        s_q, s_qsq, s_p = sem("s_q"), sem("s_qsq"), sem("s_p")
        s_h2, s_h2sq, s_h3 = sem("s_h2"), sem("s_h2sq"), sem("s_h3")
        s_h3t, s_h3tev = sem("s_h3t"), sem("s_h3tev")
        s_lg, s_lgev, s_dl, s_ex = sem("s_lg"), sem("s_lgev"), sem("s_dl"), sem("s_ex")
        s_oh, s_cum, s_cumev, s_slot = sem("s_oh"), sem("s_cum"), sem("s_cumev"), sem("s_slot")
        s_xt, s_xthi, s_xtlo = sem("s_xt"), sem("s_xthi"), sem("s_xtlo")
        s_up, s_hma, s_hmd = sem("s_up"), sem("s_hma"), sem("s_hmd")
        s_dn, s_yb = sem("s_dn"), sem("s_yb")
        s_fin = sem("s_fin")
        s_chain = sem("s_chain")
        s_pchain = sem("s_pchain")

        SET_WARM, SET_ZERO, SET_BIG = 1, 3, 6
        block = ctx.enter_context(nc.Block())

        @block.sync
        def _(sp):
            sp.dma_start(wa_sb[:, :], wa).then_inc(d_wa, 16)
            sp.dma_start(x_sb[0][:, :], x2[0]).then_inc(d_x[0], 16)
            for i in range(NT):
                sp.dma_start(gam[:, i, :], gammaT[i]).then_inc(d_gam[i], 16)
            sp.dma_start(x_sb[1][:, :], x2[1]).then_inc(d_x[1], 16)
            sp.dma_start(par[:, :], params).then_inc(d_par, 16)
            sp.dma_start(cst[:, :], consts).then_inc(d_cst, 16)
            for g in range(2):
                sp.dma_start(w1_raw[D * g:D * g + D, :, :], w1.rearrange("e d f -> d e f")).then_inc(d_w1, 16)
            sp.dma_start(w2_sb[:, :, :, :], w2.rearrange("e (c p) d -> p e c d", c=2)).then_inc(d_w2, 16)
            sp.wait_ge(s_set, SET_ZERO)
            for b in range(B):
                rows = slots_in[b].rearrange("(p r) d -> p (r d)", p=P)
                for k in range(4):
                    sp.dma_start(rows[:, k * CAP:(k + 1) * CAP], yg[b][:, 0:KS, :].rearrange("p j d -> p (j d)")).then_inc(d_zero, 16)
            for b in range(B):
                sp.wait_ge(d_scatter[b], 16 * NT)
                if b > 0:
                    sp.wait_ge(s_xt, PAIRS * b)
                src = slots_in[b].rearrange("(g e p k) d -> g e p k d", g=2, e=PAIRS, p=64)
                for p in range(PAIRS):
                    for g in range(2):
                        sp.dma_start(xb[p][64 * g:64 * g + 64, :, :, :],
                                     src[g, p].unsqueeze(2).to_broadcast([64, KS, 2, D])).then_inc(d_xb[b][p], 16)
                dst = slots_out[b].rearrange("(g e p k) d -> g e p (k d)", g=2, e=PAIRS, p=64)
                for p in range(PAIRS):
                    sp.wait_ge(s_yb, PAIRS * b + p + 1)
                    for g in range(2):
                        sp.dma_start(dst[g, p], yb_sb[64 * g:64 * g + 64, p, :, :].rearrange("p k d -> p (k d)")).then_inc(d_yb[b], 16)
            for n, (b, first, tiles) in enumerate(GROUPS):
                sp.wait_ge(s_fin, n + 1)
                for f in range(2):
                    lo, hi = f * HALF + first // 2 * P, f * HALF + (first + tiles) // 2 * P
                    sp.dma_start(out[b, lo:hi, :].rearrange("(j p) d -> p j d", p=P),
                                 fin[b][:, first + f:first + tiles:2, :]).then_inc(d_out, 16)
            sp.wait_ge(d_out, 16 * 2 * len(GROUPS))

        @block.gpsimd
        def _(pool):
            nc.gpsimd.memset(warm[:, :], 0.0).then_inc(s_set, 1)
            for b in range(B):
                nc.gpsimd.memset(yg[b][:, :, :], 0.0).then_inc(s_set, 1)
            nc.gpsimd.memset(ones[:, :], 1.0).then_inc(s_set, 1)
            nc.gpsimd.memset(ones_row[:, :], 1.0).then_inc(s_set, 1)
            nc.gpsimd.memset(big[:, :], BIG).then_inc(s_set, 1)

            def scaled_l(b, i):
                c = col_sb[b]
                pool.wait_ge(s_cl, b + 1)
                nc.gpsimd.tensor_tensor(lbc[b][:, :, :], hc[b][:, :, :], over(c[:, 21, :], D), ALU.mult).then_inc(s_lb, 1)
                pool.wait_ge(s_lb, 2 * b + 1)
                nc.gpsimd.tensor_tensor(lb[b][:, :, :], hc[b][:, :, :], over(c[:, 20, :], D), ALU.mult).then_inc(s_lb, 1)
                pool.wait_ge(s_lb, 2 * b + 2)

            def scatter(b, i):
                if b == 0:
                    pool.wait_ge(d_zero, 16 * 4 * B)
                pool.wait_ge(s_slot, b + 1)
                pool.wait_ge(s_h3, b + 1)
                for j in range(NT):
                    nc.gpsimd.indirect_dma_start(
                        slots_in[b], bass.IndirectOffsetOnAxis(ap=slot_i[b][:, j:j + 1], axis=0),
                        h3[b][:, j, :], None, bounds_check=SLOTS - 1, oob_is_err=False).then_inc(d_scatter[b], 16)

            def gather(b, i):
                pool.wait_ge(s_set, SET_ZERO)
                pool.wait_ge(d_zero, 16 * 4 * B)
                pool.wait_ge(d_yb[b], 16 * 2 * PAIRS)
                for n, (gb, first, tiles) in enumerate(GROUPS):
                    if gb != b:
                        continue
                    for j in range(first, first + tiles):
                        nc.gpsimd.indirect_dma_start(
                            yg[b][:, j, :], None, slots_out[b],
                            bass.IndirectOffsetOnAxis(ap=slot_i[b][:, j:j + 1], axis=0),
                            bounds_check=SLOTS - 1, oob_is_err=False).then_inc(d_gather[n], 16)

            def second_copy(b, i):
                pool.wait_ge(s_r, b + 1)
                nc.gpsimd.tensor_tensor(vn[b][:, :, 1, :], hc[b][:, :, :], over(col_sb[b][:, 4, :], D), ALU.mult).then_inc(s_vn2, 1)
                pool.wait_ge(s_vn2, b + 1)

            def split(b, i):
                if b > 0:
                    pool.wait_ge(s_xhi, 2 * b + i + 1)
                    nc.gpsimd.tensor_tensor(x_lo[:, hs(i)], x_sb[b][:, hs(i)], x_hi[:, hs(i)].bitcast(f32), ALU.subtract).then_inc(s_xlo, 1)
                    pool.wait_ge(s_xlo, 2 * b + i + 1)

            def retained(b, i):
                if b > 0:
                    pool.wait_ge(s_whi, 3)
                    nc.gpsimd.tensor_tensor(w1_hilo[D:P, :, :], w1_raw[D:P, :, :], w1_hilo[D:P, :, :].bitcast(f32), ALU.subtract).then_inc(s_w1lo, 1)
                    pool.wait_ge(s_w1lo, 1)

            mine = {"x": split, "retained": retained, "inverse": second_copy, "clamp": scaled_l, "slots": scatter, "gather": gather}
            for stage, b, i in ORDER:
                if stage in mine:
                    mine[stage](b, i)

        @block.scalar
        def _(act):
            fn = nc.scalar.activation

            def split(b, i):
                if b == 0 and i == 0:
                    act.wait_ge(d_wa, 16)
                    fn(wa_hilo[:, :], wa_sb[:, 0:5 * D], ACT.Copy).then_inc(s_whi, 1)
                act.wait_ge(d_x[b], 16)
                if b > 0:
                    act.wait_ge(s_proj, 5 * b)
                fn(x_hi[:, hs(i)], x_sb[b][:, hs(i)], ACT.Copy).then_inc(s_xhi, 1)

            def proj(b, i):
                if i == 4:
                    return
                act.wait_ge(s_proj, 5 * b + i + 1)
                dst, bias = (q_hi, ACOL["bq"][0]) if i % 2 == 0 else (k_hilo, ACOL["bk"][0])
                fn(dst[:, hs(i // 2)], S[UNITS[b, "proj", i] % 3], ACT.Identity, bias=wa_sb[:, bias:bias + 1]).then_inc(s_hi, 1)

            def retained(b, i):
                act.wait_ge(s_gv, NT * (b + 1))
                fn(ret[b][:, :], R[:, :], ACT.Copy).then_inc(s_ret, 1)
                if b == 0:
                    act.wait_ge(d_par, 16)
                    fn(dx_hilo[:, :], pcol("dxt"), ACT.Copy).then_inc(s_whi, 1)
                else:
                    act.wait_ge(d_w1, 32)
                    fn(w1_hilo[:, :, :], w1_raw, ACT.Copy).then_inc(s_whi, 1)

            def half_root(b, k):
                c = col_sb[b]
                act.wait_ge(s_var[k], b + 1)
                fn(c[:, 30 + k, :], c[:, 25 + k, :], ACT.Sqrt, scale=0.25).then_inc(s_root[k], 1)

            def centre(b, i):
                act.wait_ge(s_hc, b + 1)
                fn(sq[b][:, :, :], hc[b][:, :, :], ACT.Square).then_inc(s_hsq, 1)

            def norm(b, k):
                half_root(b, k)

            def vt(b, i):
                act.wait_ge(s_vt, 2 * b + i + 1)
                fn(vh[b][:, hs(i)], ABh[b][i], ACT.Copy).then_inc(s_vhi, 1)

            def dx(b, n):
                act.wait_ge(s_dx, 4 * b + n + 1)
                fn(w[b][:, n % 2, hs(n // 2)], DXB[b][n], ACT.Relu).then_inc(s_u, 1)

            def turned(b, g):
                act.wait_ge(s_wt, 4 * b + g + 1)
                tiles = 2 if g < 3 else 1
                fn(wT[b][:, 2 * g:2 * g + tiles, :].rearrange("p j n -> p (j n)"),
                   ABh[b][g % 2][:, 0:tiles * 2 * P], ACT.Copy).then_inc(s_wtev, 1)

            def aT_(b, i):
                act.wait_ge(s_a, b + 1)
                fn(aT2[b][:, :], M0[b][:, :], ACT.Square).then_inc(s_aev, 1)
                fn(aT[b][:, :], M0[b][:, :], ACT.Copy).then_inc(s_aev, 1)
                half_root(b, 2)

            def q(b, i):
                if i == 0:
                    act.wait_ge(s_q, b + 1)
                    fn(sq[b][:, :, :].rearrange("p j d -> p (j d)"), M3[b][:, :], ACT.Square).then_inc(s_qsq, 1)
                else:
                    half_root(b, 3)

            def h2(b, i):
                act.wait_ge(s_h2, b + 1)
                fn(sq[b][:, :, :], h2c[b][:, :, :], ACT.Square).then_inc(s_h2sq, 1)

            def h3_(b, i):
                half_root(b, 4)
                act.wait_ge(s_h3t, b + 1)
                fn(h3T[b][:, :], ABh[b][0], ACT.Copy).then_inc(s_h3tev, 1)

            act.wait_ge(s_set, SET_WARM)
            fn(junk[:, :], warm[:, 0:1], ACT.Sqrt)
            def slots_split(b, p):
                n = PAIRS * b + p
                act.wait_ge(s_xt, n + 1)
                if n >= 2:
                    act.wait_ge(s_up, 4 * n - 4)
                fn(xbT_hi[:, n % 2, :, :, :].rearrange("d k g s -> d (k g s)"), XTB, ACT.Copy).then_inc(s_xthi, 1)

            def up(b, p):
                n = PAIRS * b + p
                for g in range(2):
                    act.wait_ge(s_up, 4 * n + 2 * g + 1)
                    if n >= 2:
                        act.wait_ge(s_dn, n - 1)
                    a = PCOL["b1"][0] + 2 * (p + PAIRS * g)
                    fn(hm[:, n % 2, g, 0, :], UPB[b][2 * g][:, 0:CAP], ACT.Relu, bias=par[:, a:a + 1]).then_inc(s_hma, 1)

            def slots(b, i):
                if b == B - 1:
                    for a in range(B):
                        act.wait_ge(s_dl, a + 1)
                        fn(ex[a][:, :, :], lg[a][:, :, :], ACT.Exp).then_inc(s_ex, 1)

            mine = {"x": split, "proj": proj, "retained": retained, "centre": centre, "norm": norm, "vt": vt, "dx": dx, "wt": turned,
                    "aT": aT_, "q": q, "h2": h2, "h3": h3_, "slots": slots, "xt": slots_split, "up": up}
            for stage, b, i in ORDER:
                if stage in mine:
                    mine[stage](b, i)

        @block.vector
        def _(dve):
            count = [0]

            def link(ins):
                count[0] += 1
                ins.then_inc(s_chain, 1)
                dve.wait_ge(s_chain, count[0])

            tt, tsc, stt = nc.vector.tensor_tensor, nc.vector.tensor_scalar, nc.vector.scalar_tensor_tensor
            reduce = nc.vector.tensor_reduce

            def inverse_root(b, k, dst, signal=None):
                c = col_sb[b]
                v, half, r0, t = c[:, 25 + k, :], c[:, 30 + k, :], c[:, 35, :], c[:, 36, :]
                dve.wait_ge(s_root[k], b + 1)
                link(nc.vector.reciprocal(r0, half))
                link(tt(t, r0, v, ALU.mult))
                link(stt(t, t, 0.25, half, ALU.mult, ALU.add))
                if signal is None:
                    link(nc.vector.reciprocal(dst, t))
                else:
                    nc.vector.reciprocal(dst, t).then_inc(signal, 1)
                    dve.wait_ge(signal, b + 1)

            def low(dst, src, hi, half=slice(0, P)):
                return tt(dst[half, :], src[half, :], hi[half, :].bitcast(f32), ALU.subtract)

            upper = slice(D, P)

            def split(b, i):
                if b == 0 and i == 0:
                    dve.wait_ge(s_whi, 1)
                    low(wa_hilo[:, :], wa_sb[:, 0:5 * D], wa_hilo[:, :], upper).then_inc(s_wlo, 1)
                if b > 0:
                    return
                dve.wait_ge(s_xhi, 2 * b + i + 1)
                low(x_lo[:, hs(i)], x_sb[b][:, hs(i)], x_hi[:, hs(i)]).then_inc(s_xlo, 1)

            def proj(b, i):
                src = S[UNITS[b, "proj", i] % 3]
                if i == 4:
                    dve.wait_ge(s_proj, 5 * b + 5)
                    bv = wa_sb[:, ACOL["bv"][0]:ACOL["bv"][1]].unsqueeze(1).to_broadcast([P, NT, D])
                    tt(v_sb[:, :, :], src.rearrange("p (j d) -> p j d", d=D), bv, ALU.add).then_inc(s_v, 1)
                    return
                dve.wait_ge(s_hi, 4 * b + i + 1)
                if i % 2 == 0:
                    a = ACOL["bq"][0]
                    stt(q_lo[:, hs(i // 2)], src, wa_sb[:, a:a + 1], q_hi[:, hs(i // 2)].bitcast(f32), ALU.add, ALU.subtract).then_inc(s_lo, 1)
                else:
                    a = ACOL["bk"][0]
                    stt(k_hilo[D:P, hs(i // 2)], src[D:P, :], wa_sb[D:P, a:a + 1], k_hilo[D:P, hs(i // 2)].bitcast(f32),
                        ALU.add, ALU.subtract).then_inc(s_lo, 1)

            def score(b, i):
                s, f = divmod(i, 2)
                n = 2 * NT * b + i
                dve.wait_ge(d_gam[s], 16)
                dve.wait_ge(s_score, n + 1)
                if n >= NG:
                    dve.wait_ge(s_gv, (n - NG) // 2 + 1)
                tt(gs[:, n % NG, :], S[UNITS[b, "score", i] % 3], gam[:, s, hs(f)], ALU.mult).then_inc(s_gs, 1)

            def retained(b, i):
                if b > 0:
                    return
                dve.wait_ge(s_whi, 2)
                low(dx_hilo[:, :], pcol("dxt"), dx_hilo[:, :], upper).then_inc(s_wlo, 1)
                dve.wait_ge(d_cst, 16)
                dve.wait_ge(d_par, 16)
                nc.vector.tensor_copy(tri_bf[:, :], ccol("tri")).then_inc(s_bfc, 1)
                nc.vector.memset(ones_bf[:, :], 1.0).then_inc(s_bfc, 1)
                et = pcol("et").rearrange("p (c d) -> p c d", c=2)
                link(reduce(et_mean[:, :], et, AX, ALU.add))
                link(tsc(et_mean[:, :], et_mean[:, :], 1.0 / D, None, ALU.mult))
                tt(etc[:, :, :], et, et_mean[:, :].unsqueeze(2).to_broadcast([P, 2, D]), ALU.subtract).then_inc(s_etc, 1)

            def prelu(b, i):
                dve.wait_ge(s_mix, b + 1)
                y, below = M0[b][:, :].rearrange("p (j d) -> p j d", d=D), sq[b][:, :, :]
                link(tsc(below, y, 0.0, pcol("a"), ALU.min, ALU.mult))
                stt(h[b][:, :, :], y, 0.0, below, ALU.max, ALU.add).then_inc(s_y, 1)
                dve.wait_ge(s_y, b + 1)

            def centre(b, i):
                c = col_sb[b]
                link(reduce(c[:, 0, :], h[b][:, :, :], AX, ALU.add))
                link(tsc(c[:, 1, :], c[:, 0, :], 1.0 / D, None, ALU.mult))
                tt(hc[b][:, :, :], h[b][:, :, :], over(c[:, 1, :], D), ALU.subtract).then_inc(s_hc, 1)

            def norm(b, k):
                c = col_sb[b]
                if k == 0:
                    dve.wait_ge(s_hsq, b + 1)
                    link(reduce(c[:, 2, :], sq[b][:, :, :], AX, ALU.add))
                    tsc(c[:, 25, :], c[:, 2, :], 1.0 / D, LN_EPS, ALU.mult, ALU.add).then_inc(s_var[0], 1)
                    tsc(c[:, 3, :], c[:, 2, :], 1.0 / D, None, ALU.mult)
                    dve.wait_ge(s_var[0], b + 1)
                else:
                    link(tt(c[:, 5, :], c[:, 4, :], c[:, 4, :], ALU.mult))
                    link(tt(c[:, 5, :], c[:, 5, :], c[:, 3, :], ALU.mult))
                    tsc(c[:, 26, :], c[:, 5, :], LN_EPS, None, ALU.add).then_inc(s_var[1], 1)
                    dve.wait_ge(s_var[1], b + 1)

            def inverse(b, i):
                c = col_sb[b]
                inverse_root(b, 0, c[:, 4, :], s_r)
                tt(vn[b][:, :, 0, :], hc[b][:, :, :], over(c[:, 4, :], D), ALU.mult).then_inc(s_vn, 1)

            def vt(b, i):
                dve.wait_ge(s_vhi, 2 * b + i + 1)
                low(vl[b][:, hs(i)], ABh[b][i], vh[b][:, hs(i)]).then_inc(s_vlo, 1)

            def dx(b, n):
                if n % 2 == 0:
                    return
                f = n // 2
                dve.wait_ge(s_u, 4 * b + n + 1)
                tt(yT[b][:, 0, hs(f)], w[b][:, 0, hs(f)], w[b][:, 1, hs(f)], ALU.add).then_inc(s_us, 1)

            def usum(b, i):
                if i == 0:
                    return
                c = col_sb[b]
                inverse_root(b, 1, c[:, 6, :])
                link(tt(c[:, 7, :], c[:, 4, :], c[:, 6, :], ALU.mult))
                dve.wait_ge(s_usum, b + 1)
                cm = c[:, 8, :].rearrange("p (f j) -> p j f", f=2)
                link(tsc(cm, M3[b][:, 0:NT].rearrange("p (j f) -> p j f", f=2), 1.0 / L1_EPS, 1.0, ALU.mult, ALU.min))
                nc.vector.tensor_tensor_scan(c[:, 9, :], ones8[:, :], c[:, 8, :], 0.0, ALU.mult, ALU.add).then_inc(s_cm, 1)

            def clamp(b, i):
                c = col_sb[b]
                U = M3[b][:, 0:NT]
                M = M3[b][:, NT:2 * NT].rearrange("p (f j) -> p j f", f=2)
                dve.wait_ge(s_m, b + 1)
                link(tsc(c[:, 10, :].rearrange("p (j f) -> p j f", f=2), M, 1.0, DECAY, ALU.min, ALU.mult))
                link(tt(c[:, 10, :], U, c[:, 10, :], ALU.add))
                link(tsc(c[:, 10, :], c[:, 10, :], L1_EPS, None, ALU.max))
                nc.vector.reciprocal(c[:, 11, :], c[:, 10, :]).then_inc(s_beta, 1)
                dve.wait_ge(s_beta, b + 1)
                link(stt(c[:, 20, :], c[:, 7, :], ccol("grow"), c[:, 11, :], ALU.mult, ALU.mult))
                tsc(c[:, 21, :], c[:, 20, :], TILE_DECAY, None, ALU.mult).then_inc(s_cl, 1)
                link(tsc(c[:, 12, :], c[:, 11, :], ccol("decay"), None, ALU.mult))

            def scan(b, i):
                dve.wait_ge(s_abc, b + 1)
                lo, hi = (1, HALF) if i == 0 else (HALF, T)
                for n in range(2):
                    nc.vector.tensor_tensor_scan(w[b][:, n, lo:hi], AB[b][:, lo - 1:hi - 1], w[b][:, n, lo:hi],
                                                 w[b][:, n, lo - 1:lo], ALU.mult, ALU.add).then_inc(s_w, 1)

            def at(b, i):
                mask = ccol("upper").unsqueeze(1).to_broadcast([P, 4, P])
                dve.wait_ge(s_at, 2 * b + i + 1)
                src = (M0 if i == 0 else M3)[b][:, :].rearrange("p (j t) -> p j t", t=P)
                tt(att[b][:, 4 * i:4 * i + 4, :], src, mask, ALU.mult).then_inc(s_att, 1)

            def grow(b, i):
                dve.wait_ge(s_c, 2 * b + i + 1)
                for j in range(4 * i, min(4 * i + 4, NT - 1)):
                    products = M3[b][:, (j % 4) * 2 * D:(j % 4 + 1) * 2 * D]
                    if j == 0:
                        nc.vector.tensor_copy(state[b][:, 1, :], products).then_inc(s_st, 1)
                    else:
                        dve.wait_ge(s_st, (NT - 1) * b + j)
                        stt(state[b][:, j + 1, :], state[b][:, j, :], TILE_DECAY, products, ALU.mult, ALU.add).then_inc(s_st, 1)

            def aT_(b, i):
                c = col_sb[b]
                link(tt(c[:, 13, :], c[:, 12, :], c[:, 12, :], ALU.mult))
                dve.wait_ge(s_sa, b + 1)
                tt(c[:, 14, :], c[:, 13, :], M3[b][:, 0:NT], ALU.mult).then_inc(s_saev, 1)
                dve.wait_ge(s_saev, b + 1)
                tsc(c[:, 27, :], c[:, 14, :], 1.0 / D, LN_EPS, ALU.mult, ALU.add).then_inc(s_var[2], 1)

            def dy(b, n):
                dve.wait_ge(s_dy, 4 * b + n + 1)
                stt(yT[b][:, n % 2, hs(n // 2)], DYB[b][n], 0.0, w[b][:, n % 2, hs(n // 2)], ALU.max, ALU.mult).then_inc(s_yy, 1)

            def scale(b, i):
                c = col_sb[b]
                inverse_root(b, 2, c[:, 15, :])
                link(tt(c[:, 16, :], c[:, 12, :], c[:, 15, :], ALU.mult))
                link(tt(c[:, 16, :], c[:, 16, :], c[:, 11, :], ALU.mult))
                link(tt(c[:, 17, :], c[:, 16, :], c[:, 16, :], ALU.mult))

            def q(b, i):
                c = col_sb[b]
                if i == 0:
                    dve.wait_ge(s_qsq, b + 1)
                    link(reduce(c[:, 18, :], sq[b][:, :, :], AX, ALU.add))
                    link(tt(c[:, 18, :], c[:, 18, :], c[:, 17, :], ALU.mult))
                    tsc(c[:, 28, :], c[:, 18, :], 1.0 / D, LN_EPS, ALU.mult, ALU.add).then_inc(s_var[3], 1)
                    dve.wait_ge(s_var[3], b + 1)
                else:
                    inverse_root(b, 3, c[:, 19, :])
                    link(tt(c[:, 19, :], c[:, 19, :], c[:, 16, :], ALU.mult))
                    tt(pq[b][:, :, :], M3[b][:, :].rearrange("p (j d) -> p j d", d=D), over(c[:, 19, :], D), ALU.mult).then_inc(s_p, 1)

            def h2(b, i):
                dve.wait_ge(s_p, b + 1)
                tt(h2c[b][:, :, :], hc[b][:, :, :], pq[b][:, :, :], ALU.add).then_inc(s_h2, 1)

            def variance(b, i):
                c = col_sb[b]
                dve.wait_ge(s_h2sq, b + 1)
                link(reduce(c[:, 22, :], sq[b][:, :, :], AX, ALU.add))
                tsc(c[:, 29, :], c[:, 22, :], 1.0 / D, LN_EPS, ALU.mult, ALU.add).then_inc(s_var[4], 1)
                dve.wait_ge(s_var[4], b + 1)

            def h3_(b, i):
                c = col_sb[b]
                inverse_root(b, 4, c[:, 23, :])
                tt(h3[b][:, :, :], h2c[b][:, :, :], over(c[:, 23, :], D), ALU.mult).then_inc(s_h3, 1)

            def gates(b, i):
                c = col_sb[b]
                dve.wait_ge(s_lg, b + 1)
                gb = pcol("gb").unsqueeze(1).to_broadcast([P, NT, NE])
                tt(lg[b][:, :, :], M3[b][:, 0:NT * NE].rearrange("p (j e) -> p j e", e=NE), gb, ALU.add).then_inc(s_lgev, 1)
                dve.wait_ge(s_lgev, b + 1)
                link(reduce(c[:, 24, :], lg[b][:, :, :], AX, ALU.max))
                tt(lg[b][:, :, :], lg[b][:, :, :], over(c[:, 24, :], NE), ALU.subtract).then_inc(s_dl, 1)
                dve.wait_ge(s_dl, b + 1)
                first = ccol("first").rearrange("p (j e) -> p j e", e=NE)
                link(stt(key[b][:, :, :], lg[b][:, :, :], 0.0, first, ALU.is_equal, ALU.mult))
                link(reduce(c[:, 37, :], key[b][:, :, :], AX, ALU.max))
                tt(oh[b][:, :, :], key[b][:, :, :], over(c[:, 37, :], NE), ALU.is_equal).then_inc(s_oh, 1)
                dve.wait_ge(s_oh, b + 1)
                base = ccol("base").rearrange("p (j e) -> p j e", e=NE)
                link(tt(key[b][:, :, :], oh[b][:, :, :], base, ALU.mult))
                link(reduce(c[:, 38, :], key[b][:, :, :], AX, ALU.add))

            def slots(b, i):
                c = col_sb[b]
                dve.wait_ge(s_cum, b + 1)
                v4 = "p (j f) e -> p j f e"
                tt(key[b][:, :, :].rearrange(v4, f=2), M0[b][:, 0:NT * NE].rearrange("p (f j e) -> p j f e", f=2, e=NE),
                   oh[b][:, :, :].rearrange(v4, f=2), ALU.mult).then_inc(s_cumev, 1)
                dve.wait_ge(s_cumev, b + 1)
                link(reduce(c[:, 39, :], key[b][:, :, :], AX, ALU.add))
                link(stt(c[:, 38, :], c[:, 39, :], -1.0, c[:, 38, :], ALU.add, ALU.add))
                link(tsc(c[:, 39, :], c[:, 39, :], float(CAP), float(2 * SLOTS), ALU.is_gt, ALU.mult))
                tt(slot_i[b][:, :], c[:, 38, :], c[:, 39, :], ALU.add).then_inc(s_slot, 1)

            def probabilities(b, i):
                for b in range(B):
                    c = col_sb[b]
                    dve.wait_ge(s_ex, b + 1)
                    link(reduce(c[:, 0, :], ex[b][:, :, :], AX, ALU.add))
                    link(nc.vector.reciprocal(c[:, 2, :], c[:, 0, :]))
                    link(tt(fin[b][:, :, :], h2c[b][:, :, :], over(c[:, 1, :], D), ALU.add))

            def slots_split(b, p):
                n = PAIRS * b + p
                dve.wait_ge(s_xthi, n + 1)
                flat_ = "d k g s -> d (k g s)"
                low(xbT_lo[:, n % 2, :, :, :].rearrange(flat_), XTB, xbT_hi[:, n % 2, :, :, :].rearrange(flat_)).then_inc(s_xtlo, 1)

            def up(b, p):
                n = PAIRS * b + p
                for g in range(2):
                    dve.wait_ge(s_up, 4 * n + 2 * g + 2)
                    if n >= 2:
                        dve.wait_ge(s_dn, n - 1)
                    a = PCOL["b1"][0] + 2 * (p + PAIRS * g) + 1
                    tsc(hm[:, n % 2, g, 1, :], UPB[b][2 * g + 1][:, 0:CAP], par[:, a:a + 1], 0.0, ALU.add, ALU.max).then_inc(s_hmd, 1)

            def down(b, p):
                dve.wait_ge(s_dn, PAIRS * b + p + 1)
                if b > 0:
                    dve.wait_ge(d_yb[b - 1], 16 * 2 * PAIRS)
                a = PCOL["b2"][0] + p * D
                b2 = par[:, a:a + D].unsqueeze(1).to_broadcast([P, KS, D])
                src = DNB[b][p % len(DNB[b])].rearrange("p (k d) -> p k d", d=D)
                tt(yb_sb[:, p, :, :], src, b2, ALU.add).then_inc(s_yb, 1)

            def finish(_, n):
                b, first, tiles = GROUPS[n]
                c = col_sb[b]
                t4 = slice(first, first + tiles)
                y, pos, mask, rep = yg[b][:, t4, :], fpos[:, 0:tiles, :], fmask[:, 0:tiles, :], frep[:, 0:tiles, :]
                z = fin[b][:, t4, :]
                dve.wait_ge(d_gather[n], 16 * tiles)
                link(tt(y, y, c[:, 2, t4].unsqueeze(2).to_broadcast([P, tiles, D]), ALU.mult))
                link(tsc(pos, y, 0.0, None, ALU.max))
                link(stt(y, y, 0.0, pos, ALU.min, ALU.add))
                tsc(rep, y, 1e4, -1e4, ALU.min, ALU.max)
                link(tsc(mask, y, 0.0, 0.0, ALU.mult, ALU.is_equal))
                link(nc.vector.copy_predicated(rep, mask, y))
                tt(z, z, rep, ALU.add).then_inc(s_fin, 1)

            link(nc.vector.memset(ones8[:, :], 1.0))
            mine = {"x": split, "proj": proj, "score": score, "retained": retained, "prelu": prelu, "centre": centre, "norm": norm,
                    "inverse": inverse, "scale": scale, "variance": variance, "vt": vt, "dx": dx, "usum": usum, "clamp": clamp, "scan": scan, "at": at, "grow": grow, "aT": aT_, "dy": dy,
                    "q": q, "h2": h2, "h3": h3_, "gate": gates, "slots": slots, "prob": probabilities, "xt": slots_split,
                    "up": up, "down": down, "finish": finish}
            for stage, b, i in ORDER:
                if stage in mine:
                    mine[stage](b, i)

        @block.tensor
        def _(pe):
            mm = nc.tensor.matmul

            def bank_free(n):
                if n < 3:
                    return
                name, b, i = UNIT_LIST[n - 3]
                if name == "score":
                    pe.wait_ge(s_gs, 2 * NT * b + i + 1)
                elif i == 4:
                    pe.wait_ge(s_v, b + 1)
                else:
                    pe.wait_ge(s_lo, 4 * b + i + 1)

            def twice(dst, hilo, hi, lo):
                mm(dst, hilo, hi, start=True, stop=False)
                return mm(dst, hilo, lo, start=False, stop=True)

            def proj(b, i):
                if i == 0:
                    pe.wait_ge(s_wlo, 1)
                if i in (0, 2):
                    pe.wait_ge(s_xlo, 2 * b + i // 2 + 1)
                n = UNITS[b, "proj", i]
                bank_free(n)
                if i < 4:
                    last = twice(S[n % 3], wa_hilo[:, (i % 2) * P:(i % 2 + 1) * P], x_hi[:, hs(i // 2)], x_lo[:, hs(i // 2)])
                else:
                    wv = wa_hilo[:, 4 * D:5 * D]
                    for j in range(NT):
                        mm(S[n % 3][:, j * D:(j + 1) * D], x_hi[:, ts(j)], wv, start=True, stop=False)
                        last = mm(S[n % 3][:, j * D:(j + 1) * D], x_lo[:, ts(j)], wv, start=False, stop=True)
                last.then_inc(s_proj, 1)

            def retained_part(b, s):
                if s == 0:
                    pe.wait_ge(s_v, b + 1)
                if s == 0 and b > 0:
                    pe.wait_ge(s_ret, b)
                pe.wait_ge(s_gs, 16 * b + 2 * s + 2)
                for f in range(2):
                    last = mm(R[D * f:D * f + D, :], v_sb[:, s, :], gs[:, (16 * b + 2 * s + f) % NG, :],
                              start=(s == 0), stop=(s == NT - 1))
                last.then_inc(s_gv, 1)

            def score(b, i):
                s, f = divmod(i, 2)
                if i in (0, 1, NT):
                    pe.wait_ge(s_lo, 4 * b + {0: 2, 1: 3, NT: 4}[i])
                n = UNITS[b, "score", i]
                bank_free(n)
                twice(S[n % 3], k_hilo[:, ts(s)], q_hi[:, hs(f)], q_lo[:, hs(f)]).then_inc(s_score, 1)
                if f == 1 and s >= 1:
                    retained_part(b, s - 1)

            def retained(b, i):
                retained_part(b, NT - 1)

            def wo(b, i):
                pe.wait_ge(s_ret, b + 1)
                if b == 0:
                    pe.wait_ge(d_par, 16)
                    pe.wait_ge(d_cst, 16)
                    pe.wait_ge(s_set, SET_BIG)
                for j in range(4):
                    mm(M0[b][:, ts(j)], ret[b][:, ts(j)], pcol("wo"), start=True, stop=False)
                    last = mm(M0[b][:, ts(j)], ones_row[0:1, :], pcol("bo", 0, 1), start=False, stop=True)
                last.then_inc(s_mix, 1)

            def vt(b, i):
                pe.wait_ge(s_vn, b + 1)
                pe.wait_ge(s_vn2, b + 1)
                for tau in range(4 * i, 4 * i + 4):
                    tile = vn[b][:, place(tau), :, :].rearrange("p g d -> p (g d)")
                    last = nc.tensor.transpose(ABh[b][i][:, ts(tau % 4)], tile, ccol("ident"))
                last.then_inc(s_vt, 1)

            def dx(b, n):
                f, c = divmod(n, 2)
                if n == 0:
                    pe.wait_ge(s_wlo, 2)
                    pe.wait_ge(s_y, b + 1)
                if c == 0:
                    pe.wait_ge(s_vlo, 2 * b + f + 1)
                twice(DXB[b][n], dx_hilo[:, ts(c)], vh[b][:, hs(f)], vl[b][:, hs(f)]).then_inc(s_dx, 1)

            def usum(b, i):
                pe.wait_ge(s_us, 2 * b + i + 1)
                pe.wait_ge(s_u, 4 * b + 2)
                for tau in range(4 * i, 4 * i + 4):
                    last = mm(M3[b][:, place(tau):place(tau) + 1], yT[b][:, 0, ts(tau)], ones[:, :], start=True, stop=True)
                if i == 1:
                    last.then_inc(s_usum, 1)

            def clamp(b, i):
                pe.wait_ge(s_cm, b + 1)
                cm, run = col_sb[b][:, 8, :], col_sb[b][:, 9, :]
                mm(M3[b][:, NT:2 * NT], ccol("near"), cm, start=True, stop=False)
                mm(M3[b][:, NT + 1:2 * NT], ccol("prev"), cm[:, 0:NT - 1], start=False, stop=False)
                mm(M3[b][:, NT + 2:2 * NT], big[:, :], run[:, 0:NT - 2], start=False, stop=True).then_inc(s_m, 1)

            def beta(b, i):
                pe.wait_ge(s_beta, b + 1)
                pe.wait_ge(s_u, 4 * b + 4)
                for tau in range(NT):
                    k = place(tau)
                    last = mm(ABh[b][tau // 4][:, ts(tau % 4)], col_sb[b][:, 11, k:k + 1].to_broadcast([P, P]), ccol("ident97"),
                              start=True, stop=True)
                last.then_inc(s_abc, 1)

            def at(b, i):
                pe.wait_ge(s_w, 4 * b + 2 * i + 2)
                if i == 0:
                    pe.wait_ge(s_u, 4 * b + 1)
                if i == 1:
                    pe.wait_ge(s_beta, b + 1)
                for tau in range(4 * i, 4 * i + 4):
                    for c in range(2):
                        last = mm((M0 if i == 0 else M3)[b][:, ts(tau % 4)], w[b][:, c, ts(tau)], w[b][:, c, ts(tau)],
                                  start=(c == 0), stop=(c == 1))
                last.then_inc(s_at, 1)

            def turned(b, g):
                if g >= 2:
                    pe.wait_ge(s_wtev, 4 * b + g - 1)
                else:
                    pe.wait_ge(s_w, 4 * b + 4)
                for j in range(2 * g, min(2 * g + 2, NT - 1)):
                    for c in range(2):
                        at_ = (j % 2) * 2 * P + c * P
                        last = nc.tensor.transpose(ABh[b][g % 2][:, at_:at_ + P], w[b][:, c, ts(j)], ccol("ident"))
                last.then_inc(s_wt, 1)

            def grow(b, i):
                if i == 0:
                    pe.wait_ge(s_att, 2 * b + 2)
                    pe.wait_ge(s_lb, 2 * b + 1)
                else:
                    pe.wait_ge(s_st, (NT - 1) * b + 4)
                for j in range(4 * i, min(4 * i + 4, NT - 1)):
                    pe.wait_ge(s_wtev, 4 * b + j // 2 + 1)
                    for c in range(2):
                        lo = (j % 4) * 2 * D + c * D
                        last = mm(M3[b][:, lo:lo + D], wT[b][:, j, ts(c)], lbc[b][:, place(j), :], start=True, stop=True)
                last.then_inc(s_c, 1)

            def chunk(b, j):
                if j == 0:
                    pe.wait_ge(s_att, 2 * b + 2)
                f = j // 4
                dst = M0[b][D * f:D * f + D, ts(j % 4)]
                pe.wait_ge(s_lb, 2 * b + 2)
                last = mm(dst, lb[b][:, place(j), :], att[b][:, j, :], start=True, stop=(j == 0))
                if j > 0:
                    pe.wait_ge(s_st, (NT - 1) * b + j)
                    for c in range(2):
                        last = mm(dst, state[b][:, j, c * D:(c + 1) * D], w[b][:, c, ts(j)], start=False, stop=(c == 1))
                if j == NT - 1:
                    last.then_inc(s_a, 1)

            def aT_(b, i):
                pe.wait_ge(s_aev, 2 * b + 1)
                pe.wait_ge(s_st, (NT - 1) * (b + 1))
                for j in range(4):
                    last = mm(M3[b][:, 2 * j:2 * j + 2], aT2[b][:, ts(j)], ccol("halves"), start=True, stop=True)
                last.then_inc(s_sa, 1)

            def dy(b, n):
                f, c = divmod(n, 2)
                if n == 0:
                    pe.wait_ge(s_aev, 2 * b + 2)
                    pe.wait_ge(s_wtev, 4 * b + 4)
                if n == 3:
                    pe.wait_ge(s_yy, 4 * b + 1)
                a = PCOL["dyt"][0] + c * P
                mm(DYB[b][n], par[D * f:D * f + D, a:a + P], aT[b][D * f:D * f + D, :], start=True, stop=True).then_inc(s_dy, 1)

            def q(b, i):
                if i == 1:
                    return
                pe.wait_ge(s_etc, 1)
                pe.wait_ge(s_saev, b + 1)
                pe.wait_ge(s_yy, 4 * b + 4)
                for tau in range(NT):
                    for c in range(2):
                        k = place(tau)
                        last = mm(M3[b][:, k * D:(k + 1) * D], yT[b][:, c, ts(tau)], etc[:, c, :], start=(c == 0), stop=(c == 1))
                last.then_inc(s_q, 1)

            def h3_(b, i):
                pe.wait_ge(s_h3, b + 1)
                for j in range(4):
                    last = nc.tensor.transpose(ABh[b][0][:, ts(j)], h3[b][:, 2 * j:2 * j + 2, :].rearrange("p f d -> p (f d)"), ccol("ident"))
                last.then_inc(s_h3t, 1)

            def gates(b, i):
                pe.wait_ge(s_h3tev, b + 1)
                pe.wait_ge(s_p, b + 1)
                pe.wait_ge(s_qsq, b + 1)
                for j in range(4):
                    last = mm(M3[b][:, 2 * j * NE:(2 * j + 2) * NE], h3T[b][:, ts(j)], pcol("gate"), start=True, stop=True)
                last.then_inc(s_lg, 1)

            def slots(b, i):
                pe.wait_ge(s_bfc, 2)
                pe.wait_ge(s_oh, b + 1)
                terms = [(M0[b][:, 0:NT * NE].rearrange("p (f j e) -> p f j e", f=2, e=NE), tri_bf,
                          oh[b][:, :, :].rearrange("p (j f) e -> p f j e", f=2))]
                for tau in range(NT - 1):
                    k, n = place(tau), NT - 1 - tau
                    terms.append((M0[b][:, (tau + 1) * NE:NT * NE].rearrange("p (j e) -> p j e", e=NE), ones_bf,
                                  oh[b][:, k:k + 1, :].to_broadcast([P, n, NE])))
                for a in range(b):
                    for k in range(NT):
                        terms.append((M0[b][:, 0:NT * NE].rearrange("p (j e) -> p j e", e=NE), ones_bf,
                                      oh[a][:, k:k + 1, :].to_broadcast([P, NT, NE])))
                for n, (dst, lhs, rhs) in enumerate(terms):
                    last = mm(dst, lhs[:, :], rhs, start=(n == 0), stop=(n == len(terms) - 1))
                last.then_inc(s_cum, 1)

            pe.wait_ge(s_set, SET_WARM)
            for i in range(WARM):
                mm(M0[0][:, :], warm[:, 0:P], warm[:, :], start=True, stop=True)
            def keep_warm(b, i):
                if i == 0:
                    pe.wait_ge(s_h3tev, B)
                for k in range(WARM_BLOCK):
                    mm(ring2[:, 0:HALF], warm[:, 0:P], warm[:, :], start=True, stop=True)

            def hidden_read(unit):
                pe.wait_ge(s_hma if unit % 2 == 0 else s_hmd, unit // 2 + 1)

            def slots_turned(b, p):
                n = PAIRS * b + p
                if n == 0:
                    pe.wait_ge(s_h3tev, 1)
                elif b == 0 or p == 0:
                    hidden_read(4 * n - 3)
                    hidden_read(4 * n - 2)
                else:
                    pe.wait_ge(s_xtlo, n)
                pe.wait_ge(d_xb[b][p], 32)
                for k in range(KS):
                    tile = xb[p][:, k, :, :].rearrange("p g d -> p (g d)")
                    last = nc.tensor.transpose(XTB[:, k * P:(k + 1) * P], tile, ccol("ident"))
                last.then_inc(s_xt, 1)

            def up(b, p):
                n = PAIRS * b + p
                if p == 0:
                    pe.wait_ge(s_w1lo, 1)
                    pe.wait_ge(s_cumev, b + 1)
                    pe.wait_ge(s_lgev, b + 1)
                pe.wait_ge(s_xtlo, n + 1)
                for g in range(2):
                    for c in range(2):
                        u = 2 * g + c
                        if u == 0 and n > 0 and (b == 0 or p == 0):
                            hidden_read(4 * n - 1)
                        elif u == 3 and (b == 0 or p == 0):
                            hidden_read(4 * n if b == 0 else 4 * n - 1)
                        elif b > 0 and p > 0:
                            hidden_read(4 * n + u - 4)
                        twice(UPB[b][u][:, 0:CAP], w1_hilo[:, p + PAIRS * g, ts(c)],
                              xbT_hi[:, n % 2, :, g, :], xbT_lo[:, n % 2, :, g, :]).then_inc(s_up, 1)

            def down(b, p):
                n = PAIRS * b + p
                banks = DNB[b]
                if p == 0:
                    pe.wait_ge(d_w2, 16)
                pe.wait_ge(s_hma, 2 * n + 2)
                pe.wait_ge(s_hmd, 2 * n + 2)
                if n >= len(banks):
                    pe.wait_ge(s_yb, n - len(banks) + 1)
                for k in range(KS):
                    for c in range(2):
                        for g in range(2):
                            last = mm(banks[p % len(banks)][64 * g:64 * g + 64, k * D:(k + 1) * D], hm[:, n % 2, g, c, k * D:(k + 1) * D],
                                      w2_sb[:, p + PAIRS * g, c, :], start=(c == 0), stop=(c == 1))
                last.then_inc(s_dn, 1)

            mine = {"proj": proj, "score": score, "retained": retained, "wo": wo, "vt": vt, "dx": dx, "usum": usum, "clamp": clamp,
                    "beta": beta, "at": at, "wt": turned, "grow": grow, "chunk": chunk, "aT": aT_, "dy": dy, "q": q, "h3": h3_,
                    "gate": gates, "slots": slots, "warm": keep_warm, "xt": slots_turned, "up": up, "down": down}
            for stage, b, i in ORDER:
                if stage in mine:
                    mine[stage](b, i)


def constants(np):
    out = np.zeros((P, CWIDTH), np.float32)

    def put(name, value):
        out[:, CCOL[name][0]:CCOL[name][1]] = value
    s, t = np.arange(P)[:, None], np.arange(P)[None, :]
    put("ident", (s == t))
    put("ident97", DECAY * (s == t))
    put("upper", (s < t))
    put("tri", (s <= t))

    def power(k):
        return np.where(k >= 3, BIG, (DECAY / L1_EPS) ** np.clip(k, 0, 2).astype(np.float64))
    put("near", np.where(s < t, power(t - 1 - s), 0.0))
    put("prev", power(t - 1 - s + P))
    put("grow", DECAY ** -(s + 1.0))
    put("decay", DECAY ** (s * 1.0))
    e = np.arange(NT * NE)[None, :] % NE
    put("first", (NE - e) * np.ones((P, 1)))
    put("base", (CAP * e) * np.ones((P, 1)))
    put("halves", np.arange(2)[None, :] == s // D)
    return out


def kernel(**inputs):
    import numpy as np
    import concourse.bacc as bacc
    from concourse.bass_utils import run_bass_kernel_spmd

    g = {k: np.asarray(v) for k, v in inputs.items()}
    f = np.float32
    x = g["x"].reshape(B, T, D)
    xT = x.transpose(0, 2, 1)
    x2 = np.concatenate([xT, xT], axis=1)
    wa = np.zeros((P, AWIDTH), f)
    twice = lambda w: np.concatenate([w, w], axis=0)
    for name, value in (("wq", twice(np.concatenate([g["L0_tok_Wq"]] * 2, axis=1))), ("wk", twice(np.concatenate([g["L0_tok_Wk"]] * 2, axis=1))),
                        ("wv", twice(g["L0_tok_Wv"])), ("bq", twice(g["L0_tok_bq"])[:, None]), ("bk", twice(g["L0_tok_bk"])[:, None]),
                        ("bv", g["L0_tok_bv"][None, :])):
        wa[:, ACOL[name][0]:ACOL[name][1]] = value
    gammaT = g["L0_tok_d_gamma_batched"].T.reshape(NT, P, T)
    params = np.zeros((P, PWIDTH), f)

    def put(name, value, hi=P):
        params[0:hi, PCOL[name][0]:PCOL[name][1]] = value
    def on_both_halves(w):
        out = np.zeros((2 * w.shape[0], 2 * w.shape[1]), f)
        out[:w.shape[0], :w.shape[1]] = w
        out[w.shape[0]:, w.shape[1]:] = w
        return out
    put("wo", on_both_halves(g["L0_tok_Wo"]))
    put("gate", on_both_halves(g["L0_ffn_gate_w"]))
    put("gb", g["L0_ffn_gate_b"][None, :])
    put("bo", np.concatenate([g["L0_tok_bo"]] * 2)[None, :])
    put("dxt", np.concatenate([g["L0_attn_Dx"].T] * 2, axis=0))
    put("dyt", np.concatenate([g["L0_attn_Dy"].T] * 2, axis=0))
    put("et", g["L0_attn_E"].T.reshape(2, P, D).transpose(1, 0, 2).reshape(P, 2 * D))
    put("a", g["L0_tok_prelu_a"].reshape(1, 1))
    put("b1", g["L0_ffn_b1"].reshape(NE * 2, P).T)
    b2 = g["L0_ffn_b2"].reshape(2, 1, PAIRS * D)
    put("b2", np.broadcast_to(b2, (2, 64, PAIRS * D)).reshape(P, PAIRS * D))
    arrays = {"x2": x2, "wa": wa, "gammaT": gammaT, "params": params, "consts": constants(np), 
              "w1": g["L0_ffn_w1"], "w2": g["L0_ffn_w2"]}
    arrays = {n: np.ascontiguousarray(a, dtype=f) for n, a in arrays.items()}

    nc = bacc.Bacc("TRN2", target_bir_lowering=False, num_devices=1)
    f32 = mybir.dt.float32
    aps = {n: nc.dram_tensor(n, a.shape, f32, kind="ExternalInput").ap() for n, a in arrays.items()}
    out = nc.dram_tensor("out", (B, T, D), f32, kind="ExternalOutput").ap()
    slots_in = [nc.dram_tensor(f"slots_in{b}", (SLOTS, D), f32, kind="Internal").ap() for b in range(B)]
    slots_out = [nc.dram_tensor(f"slots_out{b}", (SLOTS, D), f32, kind="Internal").ap() for b in range(B)]
    build(nc, out=out, slots_in=slots_in, slots_out=slots_out, **aps)
    r = run_bass_kernel_spmd(nc, [arrays], core_ids=[0])
    return r.results[0]["out"]
```
